# Optimizing a Trainium2 kernel written in Bass

```python
import numpy as np
import jax
import jax.numpy as jnp

def _softmax(x, axis=-1):
    return jax.nn.softmax(x, axis=axis)

def _gelu(x):
    return jax.nn.gelu(x, approximate=True)

def _silu(x):
    return jax.nn.silu(x)

def _sigmoid(x):
    return jax.nn.sigmoid(x)

def _layernorm(x, axis=-1, eps=1e-05):
    m = jnp.mean(x, axis=axis, keepdims=True)
    v = jnp.var(x, axis=axis, keepdims=True)
    return (x - m) / jnp.sqrt(v + eps)

def _scatter_add(tgt, idx, src, axis=0):
    return tgt.at[idx].add(src)

def _segment_sum(src, seg, n):
    return jax.ops.segment_sum(src, seg, n)
kernel_name = 'mk_prb_d1_jaxref_r4_500048'

def setup_inputs(seed: int=0):
    np.random.seed(seed)
    _w = jnp.asarray

    def _L0_attn_setup():
        import jax, jax.numpy as jnp
        import numpy as np
        H = 16
        G = 16
        R = 4
        WIN = 64
        NEG = -1000000000.0
        key = jax.random.key(seed)
        ks = jax.random.split(key, 9)
        dm, D = (256, 256 // H)
        s = 0.02
        return {'x': jax.random.normal(ks[0], (1, 512, dm), dtype=jnp.float32), 'Wq': jax.random.normal(ks[1], (dm, dm), dtype=jnp.float32) * s, 'Wk': jax.random.normal(ks[2], (dm, dm), dtype=jnp.float32) * s, 'Wv': jax.random.normal(ks[3], (dm, dm), dtype=jnp.float32) * s, 'Wo': jax.random.normal(ks[4], (dm, dm), dtype=jnp.float32) * s, 'Wck': jax.random.normal(ks[5], (G * D, D), dtype=jnp.float32) * s, 'Wcv': jax.random.normal(ks[6], (G * D, D), dtype=jnp.float32) * s, 'Wg': jax.random.normal(ks[7], (D, 3), dtype=jnp.float32) * s, 'bg': jnp.zeros((3,), dtype=jnp.float32)}
    _L0_attn_in = _L0_attn_setup()

    def _L0_ffn_setup():
        import jax, jax.numpy as jnp
        import numpy as np
        B, T, D = (2, 512, 256)
        DCD = 1024
        RET = 128
        NEXP = 1024
        NKEYS = 64
        H = 4
        KPH = 8
        key = jax.random.key(seed)
        ks = jax.random.split(key, 10)
        s = lambda k, shape, scale: jax.random.normal(k, shape, jnp.float32) * scale
        return {'hidden_states': jax.random.normal(ks[0], (B, T, D), jnp.float32), 'Wg': s(ks[1], (D, DCD), 0.02), 'bg': jnp.zeros((DCD,), jnp.float32), 'Wu': s(ks[2], (D, DCD), 0.02), 'bu': jnp.zeros((DCD,), jnp.float32), 'Wd': s(ks[3], (DCD, D), 0.02), 'bd': jnp.zeros((D,), jnp.float32), 'Wq': s(ks[4], (D, RET * H), 0.02), 'keys': s(ks[5], (H, NKEYS, 2, RET // 2), 0.02), 'down_embed': s(ks[6], (NEXP, D), 0.02), 'up_embed': s(ks[7], (NEXP, D), 0.02)}
    _L0_ffn_in = _L0_ffn_setup()
    _d = {'L0_attn_x': _L0_attn_in['x'], 'L0_attn_Wq': _L0_attn_in['Wq'], 'L0_attn_Wk': _L0_attn_in['Wk'], 'L0_attn_Wv': _L0_attn_in['Wv'], 'L0_attn_Wo': _L0_attn_in['Wo'], 'L0_attn_Wck': _L0_attn_in['Wck'], 'L0_attn_Wcv': _L0_attn_in['Wcv'], 'L0_attn_Wg': _L0_attn_in['Wg'], 'L0_attn_bg': _L0_attn_in['bg'], 'L0_ffn_Wg': _L0_ffn_in['Wg'], 'L0_ffn_bg': _L0_ffn_in['bg'], 'L0_ffn_Wu': _L0_ffn_in['Wu'], 'L0_ffn_bu': _L0_ffn_in['bu'], 'L0_ffn_Wd': _L0_ffn_in['Wd'], 'L0_ffn_bd': _L0_ffn_in['bd'], 'L0_ffn_Wq': _L0_ffn_in['Wq'], 'L0_ffn_keys': _L0_ffn_in['keys'], 'L0_ffn_down_embed': _L0_ffn_in['down_embed'], 'L0_ffn_up_embed': _L0_ffn_in['up_embed']}
    _x0 = _d['L0_attn_x']
    _d['L0_attn_x'] = jax.random.normal(jax.random.fold_in(jax.random.key(seed), 1), (8, 512, 256), dtype=_x0.dtype)
    del _x0
    return _d

def reference(L0_attn_x, L0_attn_Wq, L0_attn_Wk, L0_attn_Wv, L0_attn_Wo, L0_attn_Wck, L0_attn_Wcv, L0_attn_Wg, L0_attn_bg, L0_ffn_Wg, L0_ffn_bg, L0_ffn_Wu, L0_ffn_bu, L0_ffn_Wd, L0_ffn_bd, L0_ffn_Wq, L0_ffn_keys, L0_ffn_down_embed, L0_ffn_up_embed):

    def _L0_attn_ref(x, Wq, Wk, Wv, Wo, Wck, Wcv, Wg, bg):
        import jax, jax.numpy as jnp
        import numpy as np
        H = 16
        G = 16
        R = 4
        WIN = 64
        NEG = -1000000000.0
        B, T, dm = x.shape
        D = dm // H
        scale = float(np.sqrt(D))

        def split_heads(y):
            return y.reshape(B, T, H, D).transpose(0, 2, 1, 3)
        q = split_heads(x @ Wq)
        k = split_heads(x @ Wk)
        v = split_heads(x @ Wv)
        pad = -T % G
        T_pad = T + pad
        k_pad = jnp.pad(k, ((0, 0), (0, 0), (0, pad), (0, 0)))
        v_pad = jnp.pad(v, ((0, 0), (0, 0), (0, pad), (0, 0)))
        nb = T_pad // G
        k_c = k_pad.reshape(B, H, nb, G * D) @ Wck
        v_c = v_pad.reshape(B, H, nb, G * D) @ Wcv
        pos = jnp.arange(T)
        blk_end = (jnp.arange(nb) + 1) * G
        c_ok = pos[:, None] >= blk_end[None, :]
        s_b = jnp.einsum('bhtd,bhnd->bhtn', q, k_c) / scale
        logits_c = jnp.where(c_ok, s_b, NEG)
        out_c = jnp.einsum('bhtn,bhnd->bhtd', jax.nn.softmax(logits_c, axis=-1), v_c)
        out_c = out_c * jnp.any(c_ok, axis=-1)[:, None].astype(out_c.dtype)
        r_eff = min(R, nb)
        _, top_idx = jax.lax.top_k(logits_c, r_eff)
        tok = (top_idx[..., None] * G + jnp.arange(G)).reshape(B, H, T, r_eff * G)
        tok = jnp.clip(tok, 0, T_pad - 1)
        bi = jnp.arange(B)[:, None, None, None]
        hi = jnp.arange(H)[None, :, None, None]
        k_s = k_pad[bi, hi, tok]
        v_s = v_pad[bi, hi, tok]
        allowed = tok <= pos[None, None, :, None]
        logits_s = jnp.where(allowed, jnp.einsum('bhtd,bhtnd->bhtn', q, k_s) / scale, NEG)
        out_s = jnp.einsum('bhtn,bhtnd->bhtd', jax.nn.softmax(logits_s, axis=-1), v_s)
        out_s = out_s * jnp.any(allowed, axis=-1)[..., None].astype(out_s.dtype)
        wmask = (jnp.abs(pos[:, None] - pos[None, :]) <= WIN // 2) & (pos[:, None] >= pos[None, :])
        logits_l = jnp.where(wmask, jnp.einsum('bhtd,bhsd->bhts', q, k) / scale, NEG)
        out_l = jnp.einsum('bhts,bhsd->bhtd', jax.nn.softmax(logits_l, axis=-1), v)
        gates = jax.nn.softmax(q.mean(axis=1) @ Wg + bg, axis=-1)

        def merge(o):
            return o.transpose(0, 2, 1, 3).reshape(B, T, dm)
        out = gates[..., 0:1] * merge(out_c) + gates[..., 1:2] * merge(out_s) + gates[..., 2:3] * merge(out_l)
        return out @ Wo

    def _L0_ffn_ref(hidden_states, Wg, bg, Wu, bu, Wd, bd, Wq, keys, down_embed, up_embed):
        import jax, jax.numpy as jnp
        import numpy as np
        B, T, D = (2, 512, 256)
        DCD = 1024
        RET = 128
        NEXP = 1024
        NKEYS = 64
        H = 4
        KPH = 8
        b, t, d = hidden_states.shape
        q = (hidden_states @ Wq).reshape(b, t, 2, H, RET // 2)
        sim = jnp.einsum('btphn,hkpn->pbthk', q, keys)
        sc, ix = jax.lax.top_k(sim, KPH)
        sx, sy = (sc[0], sc[1])
        ixx, ixy = (ix[0], ix[1])
        all_sc = (sx[..., :, None] + sy[..., None, :]).reshape(b, t, H, KPH * KPH)
        all_ix = (ixx[..., :, None] * NKEYS + ixy[..., None, :]).reshape(b, t, H, KPH * KPH)
        scores, pk = jax.lax.top_k(all_sc, KPH)
        idx = jnp.take_along_axis(all_ix, pk, axis=-1)
        de = down_embed[idx]
        ue = up_embed[idx]
        w = jnp.einsum('btd,bthkd->bthk', hidden_states, de)
        w = jax.nn.silu(w) * jax.nn.softmax(scores, axis=-1)
        experts_states = jnp.einsum('bthk,bthkd->btd', w, ue)
        mlp = jax.nn.silu(hidden_states @ Wg + bg) * (hidden_states @ Wu + bu) @ Wd + bd
        return mlp + experts_states
    x = L0_attn_x
    xn = _layernorm(x, axis=-1)
    x = x + _L0_attn_ref(xn, L0_attn_Wq, L0_attn_Wk, L0_attn_Wv, L0_attn_Wo, L0_attn_Wck, L0_attn_Wcv, L0_attn_Wg, L0_attn_bg) + _L0_ffn_ref(xn, L0_ffn_Wg, L0_ffn_bg, L0_ffn_Wu, L0_ffn_bu, L0_ffn_Wd, L0_ffn_bd, L0_ffn_Wq, L0_ffn_keys, L0_ffn_down_embed, L0_ffn_up_embed)
    return x

_drawn_inputs = setup_inputs


def setup_inputs(seed=0):
    import zlib

    import numpy as np

    out = dict(_drawn_inputs(seed))
    spreads = {'L0_attn_bg': (0.0, 0.8),
     'L0_ffn_bg': (0.0, 0.705),
     'L0_ffn_bu': (0.0, 0.697),
     'L0_ffn_bd': (0.0, 0.1)}
    factors = {'L0_attn_Wq': 8.0,
     'L0_attn_Wk': 8.0,
     'L0_attn_Wv': 5.338,
     'L0_attn_Wo': 5.287,
     'L0_attn_Wck': 8.0,
     'L0_attn_Wcv': 8.0,
     'L0_attn_Wg': 8.0,
     'L0_ffn_Wq': 8.0,
     'L0_ffn_keys': 8.0,
     'L0_ffn_down_embed': 5.531,
     'L0_ffn_up_embed': 5.441}
    for name, (base, spread) in spreads.items():
        noise = np.random.default_rng([zlib.crc32(name.encode()), seed]).standard_normal(out[name].shape)
        drawn = base * np.exp(spread * noise) if base else spread * noise
        out[name] = jnp.asarray(drawn.astype(out[name].dtype))
    for name, factor in factors.items():
        out[name] = (out[name] * factor).astype(out[name].dtype)
    return out
```

```python
import concourse.bass as bass
from concourse import mybir
from contextlib import ExitStack

F32 = mybir.dt.float32
BF16 = mybir.dt.bfloat16
ALU = mybir.AluOpType
ACT = mybir.ActivationFunctionType
AX = mybir.AxisListType

B, T, C = 8, 512, 256
H, D, BLK = 16, 16, 16
NB = T // BLK
WIN = 32
P = 128
TT = T // P
HG = 4
G = H // HG
UNITS = B * G
FF = 1024
FT = FF // P
EX = 1024
XK = EX // 64
PH = 4
KEYS = 64
NEG = -1.0e30
NOT_YET = -1.0e9
LOWEST = -3.0e38
TAKEN = 1.0e30
VW = D + 1


class Signal:

    def __init__(self, sem, per, ahead=False):
        self.sem, self.per, self.ahead = sem, per, ahead

    def at(self, turn, n=None):
        return turn.count(self.per, (self.per if n is None else n) + (self.per if self.ahead else 0))

    def before(self, turn, n=None):
        assert self.ahead
        return turn.count(self.per, self.per if n is None else n)


class Turn:

    def __init__(self, pair, half, step=0, tail=False):
        self.pair, self.half, self.index = pair, half, pair * 2 + half
        self.step, self.tail = self if step == 0 else step, tail

    def count(self, per, n):
        return self.pair * (2 * per) + (self.half * per + n)

    def next(self):
        return Turn(self.pair + self.half, 1 - self.half, step=self)


class Chain:

    def __init__(self, eng, sem, per):
        self.eng, self.sem, self.per, self.n, self.turn = eng, sem, per, 0, None

    def start(self, turn):
        self.turn, self.n = turn, 0

    def link(self, ins):
        self.n += 1
        ins.then_inc(self.sem, 1)
        self.eng.wait_ge(self.sem, self.n if self.turn is None else self.turn.count(self.per, self.n))

    def end(self):
        assert self.n == self.per, f"{self.sem}: {self.n} links in a pass, {self.per} declared"


class Banks:

    def __init__(self, banks, full, free, jobs, front=()):
        self.banks, self.full, self.free, self.jobs, self.front = banks, full, free, jobs, set(front)

    def place(self, job):
        i = self.jobs.index(job)
        return i % len(self.banks), i // len(self.banks)

    def _value(self, turn, job):
        k, before = self.place(job)
        mine = self.jobs[k::len(self.banks)]
        ahead = [j for j in mine if j in self.front]
        if turn.step is None:
            return ahead.index(job) + 1
        if turn.step.tail:
            before = [j for j in mine if j not in self.front].index(job)
        return turn.step.count(len(mine), len(ahead) + before + 1)

    def bank(self, job):
        return self.banks[self.place(job)[0]]

    def wait_free(self, eng, turn, job):
        eng.wait_ge(self.free[self.place(job)[0]], self._value(turn, job))

    def wait_full(self, eng, turn, job):
        eng.wait_ge(self.full[self.place(job)[0]], self._value(turn, job))

    def wait_read(self, eng, turn, job):
        eng.wait_ge(self.free[self.place(job)[0]], self._value(turn, job) + 1)

    def filled(self, job, ins):
        ins.then_inc(self.full[self.place(job)[0]], 1)

    def released(self, job, ins):
        ins.then_inc(self.free[self.place(job)[0]], 1)


def row(ap, index):
    if isinstance(index, int):
        return ap[index]
    names = "abcdef"[:len(ap.shape) - 1]
    return ap[bass.ds(index, 1)].rearrange(f"o {' '.join(names)} -> (o {names[0]}) {' '.join(names[1:])}")


def build(nc, x, Wq, Wk, Wv, Wo, Wck, Wcv, Wg, bg, Fg, fbg, Fu, fbu, Fd, fbd, Rq, keys, down, up, out):
    def dram(name, shape, dt=F32):
        return nc.dram_tensor(name, shape, dt, kind="Internal").ap()

    s_xt = dram("s_xt", [B, P, 2, T])
    s_qf = dram("s_qf", [B, G, 64, T])
    s_qs = dram("s_qs", [B, H, 3, D, T], BF16)
    s_ks = dram("s_ks", [B, H, 3, D, T], BF16)
    s_v = dram("s_v", [B, TT, P, H * VW])
    s_kc = dram("s_kc", [B, G, 64, HG * NB])
    s_vc = dram("s_vc", [B, G, P, HG * D])
    s_gt = dram("s_gt", [B, P, TT * 3])
    s_o = dram("s_o", [UNITS, TT, P, HG * D])
    s_y = dram("s_y", [UNITS, P, C])

    outer = ExitStack()
    with outer:
        def make(stack):
            def sb(name, shape, dt=F32):
                return stack.enter_context(nc.sbuf_tensor(name, shape, dt))

            def ps(name, shape, dt=F32):
                return stack.enter_context(nc.psum_tensor(name, shape, dt))

            def sem(name):
                return stack.enter_context(nc.semaphore(name))
            return sb, ps, sem

        sb, ps, sem = make(outer)
        ident = sb("ident", [P, P])
        identb = sb("identb", [P, P], BF16)
        causal_ts = sb("causal_ts", [P, P], BF16)
        causal_st = sb("causal_st", [P, 64], BF16)
        window_ts = sb("window_ts", [P, TT, 64], BF16)
        window_st = sb("window_st", [P, P], BF16)
        window_off = sb("window_off", [P, 32], BF16)
        onehot = sb("onehot", [P, HG, T], BF16)
        headones = sb("headones", [P, HG, P], BF16)
        onesb = sb("onesb", [P, P], BF16)
        block_ok = sb("block_ok", [P, TT, NB])
        block_no = sb("block_no", [P, TT, NB])
        any_ok = sb("any_ok", [P, TT])
        head_rows = sb("head_rows", [P, 8])
        quad_rows = sb("quad_rows", [P, HG])
        wfg = sb("wfg", [P, 2, FF])
        wfu = sb("wfu", [P, 2, FF])
        wfd = sb("wfd", [P, FT, C])
        wdn = sb("wdn", [P, 2, EX])
        wup = sb("wup", [P, EX // P, C])
        wsim = sb("wsim", [P, 2, 2 * PH * KEYS])
        bias3 = sb("bias3", [3, 2, FF], BF16)
        bdb = sb("bdb", [P, C])
        pad = sb("pad", [P, 4])
        go = sem("go")

        projecting = outer.enter_context(ExitStack())
        sb, _, _ = make(projecting)
        wq = sb("wq", [P, 2, C])
        wk = sb("wk", [P, 2, C])
        wv = sb("wv", [P, 2, C])
        wck = sb("wck", [P, BLK, P])
        wcv = sb("wcv", [P, BLK, P])
        wgate = sb("wgate", [P, 2, 3])
        bgb = sb("bgb", [P, 3])

        inner = ExitStack()
        with inner:
            sb, ps, sem = make(inner)
            wg8 = sb("wg8", [P, 3])
            wqT = sb("wqT", [P, 2, C])
            rq = sb("rq", [P, 2, 512])
            rqT = sb("rqT", [64, 8, C])
            kn = sb("kn", [P, 2, P])
            kT = sb("kT", [64, 2, C])
            dn = sb("dn", [P, EX // P, C])
            b1 = sb("b1", [1, 2, FF])
            b2 = sb("b2", [1, 2, FF])
            b3 = sb("b3", [1, 2, FF], BF16)
            b4 = sb("b4", [1, 2, FF], BF16)
            b5 = sb("b5", [1, 2, FF], BF16)
            bank = [ps(f"sbank{i}", [P, 512]) for i in range(4)]
            loaded = sem("loaded")
            diag = sem("diag")
            rows3 = sem("rows3")
            cleared = sem("cleared")
            pool_chain = sem("pool_chain_s")
            dve_chain = sem("dve_chain_s")
            pe_full = sem("pe_full_s")
            read = sem("read_s")
            split = sem("split_s")
            identity = sem("identity_s")

            block = inner.enter_context(nc.Block())

            @block.sync
            def _(sp):
                for dst, src in (
                        (wq[:, :, :], Wq.rearrange("(a p) n -> p a n", p=P)),
                        (wk[:, :, :], Wk.rearrange("(a p) n -> p a n", p=P)),
                        (wv[:, :, :], Wv.rearrange("(a p) n -> p a n", p=P)),
                        (rq[:, :, :], Rq.rearrange("(a p) n -> p a n", p=P)),
                        (kn[:, :, :], keys.rearrange("(a h) k p n -> (h k) a (p n)", a=2)),
                        (dn[:, :, :], down.rearrange("(a p) n -> p a n", p=P)),
                        (b1[:, 0, :], fbg.rearrange("(o n) -> o n", o=1)),
                        (b1[:, 1, :], fbu.rearrange("(o n) -> o n", o=1)),
                        (wfg[:, :, :], Fg.rearrange("(a p) n -> p a n", p=P)),
                        (wfu[:, :, :], Fu.rearrange("(a p) n -> p a n", p=P)),
                        (wfd[:, :, :], Fd.rearrange("(a p) n -> p a n", p=P)),
                        (wup[:, :, :], up.rearrange("(a p) n -> p a n", p=P)),
                        (bdb[:, :], fbd.rearrange("(o n) -> o n", o=1).broadcast_to([P, C])),
                        (bgb[:, :], bg.rearrange("(o n) -> o n", o=1).broadcast_to([P, 3]))):
                    sp.dma_start(dst, src).then_inc(loaded, 16)
                for h in range(8):
                    sp.dma_start(wg8[16 * h:16 * h + 16, :], Wg).then_inc(loaded, 16)
                sp.wait_ge(cleared, 2)
                for dst, src in ((wck, Wck), (wcv, Wcv)):
                    for h in range(8):
                        sp.dma_start(dst[16 * h:16 * h + 16, :, 16 * h:16 * h + 16],
                                     src.rearrange("(j d) e -> d j e", d=D)).then_inc(diag, 16)
                sp.wait_ge(split, 1)
                for r, part in enumerate((b3, b4, b5)):
                    sp.dma_start(bias3[r:r + 1, :, :], part[:, :, :]).then_inc(rows3, 16)
                sp.wait_ge(diag, 16 * 16)
                sp.wait_ge(rows3, 16 * 3)

            @block.gpsimd
            def _(pool):
                ch = Chain(pool, pool_chain, 0)
                g = nc.gpsimd

                def keep(ap, pattern, base, cm, fill, op=ALU.is_ge):
                    ch.link(g.affine_select(out=ap, in_=ap, compare_op=op, fill=fill, base=base,
                                            pattern=pattern, channel_multiplier=cm))
                g.memset(wck[:, :, :], 0.0).then_inc(cleared, 1)
                g.memset(wcv[:, :, :], 0.0).then_inc(cleared, 1)
                for m in (ident, identb):
                    ch.link(g.memset(m[:, :], 0.0))
                    g.affine_select(out=m[:, :], in_=m[:, :], compare_op=ALU.not_equal, fill=1.0, base=0,
                                    pattern=[[-1, P]], channel_multiplier=1).then_inc(identity, 1)
                g.memset(onesb[:, :], 1.0)
                for m in (causal_ts, causal_st, window_st, window_off):
                    g.memset(m[:, :], 0.0)
                ch.link(g.memset(window_ts[:, :, :], 0.0))
                keep(causal_ts[:, 0:64], [[-1, 64]], 0, 1, NEG)
                keep(causal_st[:, :], [[1, 64]], 0, -1, NEG)
                keep(window_st[:, :], [[1, P]], 0, -1, NEG)
                keep(window_st[:, :], [[-1, P]], WIN, 1, NEG)
                keep(window_off[96:128, :], [[-1, 32]], 0, 1, NEG)
                g.memset(onehot[:, :, :], 0.0)
                ch.link(g.memset(headones[:, :, :], 0.0))
                for q in range(4):
                    rows = slice(32 * q, 32 * q + 32)
                    g.memset(headones[rows, q, :], 1.0)
                    ch.link(g.memset(onehot[rows, q, :], 1.0))
                for m in (block_ok, any_ok, head_rows, quad_rows):
                    g.memset(m[:], 1.0)
                ch.link(g.memset(block_no[:, :, :], 0.0))
                for q in range(4):
                    rows = slice(32 * q, 32 * q + 32)
                    keep(window_ts[rows, :, :], [[0, TT], [1, 64]], 0, -1, NEG)
                    keep(window_ts[rows, :, :], [[0, TT], [-1, 64]], WIN, 1, NEG)
                    keep(onehot[rows, q, :], [[1, T]], 0, -BLK, 0.0)
                    keep(onehot[rows, q, :], [[-1, T]], BLK - 1, BLK, 0.0)
                    keep(onehot[rows, q, :], [[0, T]], 30, -1, 1.0)
                ch.link(g.memset(window_ts[0:32, 0, 0:32], NEG))
                keep(block_ok[:, :, :], [[P, TT], [-BLK, NB]], -BLK, 1, 0.0)
                keep(block_no[:, :, :], [[P, TT], [-BLK, NB]], -BLK, 1, NOT_YET)
                keep(any_ok[:, :], [[P, TT]], -BLK, 1, 0.0)
                keep(head_rows[:, :], [[-16, 8]], 0, 1, 0.0)
                keep(head_rows[:, :], [[16, 8]], 15, -1, 0.0)
                keep(quad_rows[:, :], [[-32, HG]], 0, 1, 0.0)
                keep(quad_rows[:, :], [[32, HG]], 31, -1, 0.0)

            jobs = ([("wqT", h) for h in range(2)] + [("rqT", i) for i in range(4)] + [("kT", 0)]
                    + [("dn", c, n) for c in range(2) for n in range(2)] + [("wgate",)]
                    + [("wsim", c) for c in range(2)])

            @block.tensor
            def _(pe):
                pe.wait_ge(loaded, 22 * 16)
                pe.wait_ge(identity, 2)
                for i, job in enumerate(jobs):
                    b = bank[i % 4]
                    if i >= 4:
                        pe.wait_ge(read, i - 3)
                    if job[0] == "wgate":
                        pe.wait_ge(read, 2)
                    if job[0] == "wsim":
                        pe.wait_ge(read, 7)
                    if job[0] == "wqT":
                        for c in range(2):
                            last = nc.tensor.transpose(b[:, c * P:c * P + P], wq[:, c, job[1] * P:job[1] * P + P], ident[:, :])
                    elif job[0] == "rqT":
                        for k in range(2):
                            for c in range(2):
                                o = 64 * (2 * job[1] + k)
                                last = nc.tensor.transpose(b[0:64, (2 * k + c) * P:(2 * k + c + 1) * P],
                                                           rq[:, c, o:o + 64], ident[:, :])
                    elif job[0] == "kT":
                        for p in range(2):
                            for a in range(2):
                                last = nc.tensor.transpose(b[0:64, (2 * p + a) * P:(2 * p + a + 1) * P],
                                                           kn[:, a, 64 * p:64 * p + 64], ident[:, :])
                    elif job[0] == "dn":
                        _n, c, n = job
                        for e in range(4):
                            last = nc.tensor.transpose(b[:, e * P:e * P + P],
                                                       dn[:, 4 * n + e, c * P:c * P + P], ident[:, :])
                    elif job[0] == "wgate":
                        for c in range(2):
                            for h in range(2):
                                last = nc.tensor.matmul(b[:, 4 * c:4 * c + 3], wqT[:, h, c * P:c * P + P],
                                                        wg8[:, :], start=(h == 0), stop=(h == 1))
                    else:
                        for i8 in range(8):
                            p, h = divmod(i8, PH)
                            last = nc.tensor.matmul(b[:, 64 * i8:64 * i8 + 64],
                                                    rqT[:, i8, job[1] * P:job[1] * P + P],
                                                    kT[:, p, 64 * h:64 * h + 64], start=True, stop=True)
                    last.then_inc(pe_full, 1)

            @block.vector
            def _(dve):
                ch = Chain(dve, dve_chain, 0)
                v = nc.vector
                dve.wait_ge(loaded, 22 * 16)
                ch.link(v.tensor_copy(b3[:, :, :], b1[:, :, :]))
                ch.link(v.tensor_tensor(b2[:, :, :], b1[:, :, :], b3[:, :, :], ALU.subtract))
                ch.link(v.tensor_copy(b4[:, :, :], b2[:, :, :]))
                v.tensor_tensor(b5[:, :, :], b2[:, :, :], b4[:, :, :], ALU.subtract).then_inc(split, 1)
                for i, job in enumerate(jobs):
                    b = bank[i % 4]
                    dve.wait_ge(pe_full, i + 1)
                    if job[0] == "wqT":
                        last = v.tensor_copy(wqT[:, job[1], :], b[:, 0:C])
                    elif job[0] == "rqT":
                        last = v.tensor_copy(rqT[:, 2 * job[1]:2 * job[1] + 2, :],
                                             b[0:64, :].rearrange("p (k n) -> p k n", k=2))
                    elif job[0] == "kT":
                        last = v.tensor_copy(kT[:, :, :], b[0:64, :].rearrange("p (k n) -> p k n", k=2))
                    elif job[0] == "dn":
                        last = v.tensor_copy(wdn[:, job[1], job[2] * 512:job[2] * 512 + 512], b[:, :])
                    elif job[0] == "wgate":
                        last = v.tensor_scalar(wgate[:, :, :], b[:, 0:8].rearrange("p (a n) -> p a n", a=2)[:, :, 0:3],
                                               1.0 / H, None, ALU.mult)
                    else:
                        last = v.tensor_copy(wsim[:, job[1], :], b[:, :])
                    last.then_inc(read, 1)

        inner = ExitStack()
        with inner:
            sb, ps, sem = make(inner)
            xin = sb("xin", [P, 2, TT, C])
            stats = sb("stats", [P, TT, 6])
            mv = sb("mv", [P, TT, 2])
            std = sb("std", [P, TT])
            rstd = sb("rstd", [P, TT])
            eps = sb("eps", [P, 1])
            xn = sb("xn", [P, TT, C])
            xT = sb("xT", [P, 2, 2, T])
            qk = sb("qk", [P, 2, 2, T])
            rem = sb("rem", [P, 2, 2, T])
            parts = sb("parts", [P, 2, 3, 2, T], BF16)
            vn = sb("vn", [P, TT, C])
            vo = sb("vo", [P, TT, H, VW])
            vT = sb("vT", [P, 2, T])
            kcs = sb("kcs", [P, 2, 8, NB])
            vcr = sb("vcr", [P, 2, HG, NB])
            vcs = sb("vcs", [P, 2, 2, HG, D])
            gl = sb("gl", [P, TT, 3])
            gm = sb("gm", [P, TT])
            gs = sb("gs", [P, TT])
            NBK = 8
            banks = [ps(f"tbank{i}", [P, 512]) for i in range(NBK)]
            R = Banks(banks, [sem(f"t_full{i}") for i in range(NBK)], [sem(f"t_free{i}") for i in range(NBK)],
                      ["x0", "x1", "q0", "q1", "k0", "k1", "v0", "v1", "w0", "w1", "kv", "gt", "vc"])
            x_in = [sem("x_in0"), sem("x_in1")]
            var_ready = Signal(sem("var_ready"), 1)
            std_ready = Signal(sem("std_ready"), 1)
            xn_ready = Signal(sem("xn_ready"), 4, ahead=True)
            part_hi = Signal(sem("part_hi"), 2)
            part_mid = Signal(sem("part_mid"), 2)
            part_lo = Signal(sem("part_lo"), 2, ahead=True)
            rem_hi = Signal(sem("rem_hi"), 2)
            rem_mid = Signal(sem("rem_mid"), 2)
            kc_ready = Signal(sem("kc_ready"), 2)
            gate_in = Signal(sem("gate_in"), 1)
            gate_exp = Signal(sem("gate_exp"), 1)
            gate_ready = Signal(sem("gate_ready"), 1)
            stored = {n: Signal(sem(f"st_{n}"), 16 * k, ahead=True) for n, k in
                      (("xt", 1), ("qf", 4), ("parts", 12), ("v", 1), ("kc", 4), ("vc", 2), ("gt", 1))}
            dve_chain = sem("dve_chain_t")
            armed = sem("armed_t")
            constants = sem("constants_t")

            block = inner.enter_context(nc.Block())

            @block.sync
            def _(sp):
                xv = x.rearrange("b (i p) c -> b p i c", p=P)
                sp.dma_start(xin[:, 0, :, :], xv[0]).then_inc(x_in[0], 16)
                sp.wait_ge(armed, 1)

                def turn(t, load_next=True):
                    i = t.index
                    if load_next:
                        sp.wait_ge(xn_ready.sem, xn_ready.before(t))
                        nxt = 1 - t.half
                        sp.dma_start(xin[:, nxt, :, :], row(xv, i + 1)).then_inc(x_in[nxt], 16)
                    R.wait_read(sp, t, "x0")
                    R.wait_read(sp, t, "x1")
                    sp.dma_start(row(s_xt, i), xT[:, t.half, :, :]).then_inc(stored["xt"].sem, 16)
                    R.wait_read(sp, t, "q0")
                    R.wait_read(sp, t, "q1")
                    for h in range(2):
                        for gg in range(2):
                            sp.dma_start(row(s_qf, i)[2 * h + gg], qk[64 * gg:64 * gg + 64, 0, h, :])\
                              .then_inc(stored["qf"].sem, 16)
                    for a, dst in ((0, s_qs), (1, s_ks)):
                        sp.wait_ge(part_lo.sem, part_lo.at(t, a + 1))
                        for h in range(2):
                            for r in range(3):
                                sp.dma_start(row(dst, i)[8 * h:8 * h + 8, r, :, :], parts[:, a, r, h, :])\
                                  .then_inc(stored["parts"].sem, 16)
                    R.wait_read(sp, t, "v0")
                    R.wait_read(sp, t, "v1")
                    sp.dma_start(row(s_v, i).rearrange("i p n -> p i n"),
                                 vo[:, :, :, :].rearrange("p i h d -> p i (h d)")).then_inc(stored["v"].sem, 16)
                    sp.wait_ge(kc_ready.sem, kc_ready.at(t))
                    for h in range(2):
                        for gg in range(2):
                            sp.dma_start(row(s_kc, i)[2 * h + gg],
                                         kcs[64 * gg:64 * gg + 64, h, HG * gg:HG * gg + HG, :]
                                         .rearrange("p h n -> p (h n)")).then_inc(stored["kc"].sem, 16)
                    sp.wait_ge(gate_ready.sem, gate_ready.at(t))
                    sp.dma_start(row(s_gt, i), gl[:, :, :].rearrange("p i n -> p (i n)")).then_inc(stored["gt"].sem, 16)
                    R.wait_read(sp, t, "vc")
                    for h in range(2):
                        sp.dma_start(row(s_vc, i)[2 * h:2 * h + 2].rearrange("g p n -> p g n"),
                                     vcs[:, h, :, :, :].rearrange("p g h d -> p g (h d)"))\
                          .then_inc(stored["vc"].sem, 16)

                with sp.Fori(0, B // 2 - 1) as w:
                    turn(Turn(w, 0))
                    turn(Turn(w, 1))
                turn(Turn(B // 2 - 1, 0))
                turn(Turn(B // 2 - 1, 1), load_next=False)
                for s in stored.values():
                    sp.wait_ge(s.sem, s.per * (B + 1))

            @block.gpsimd
            def _(pool):
                g = nc.gpsimd
                for s in (xn_ready, part_lo, *stored.values()):
                    pool.sem_inc(s.sem, s.per)
                for s in R.free:
                    pool.sem_inc(s, 1)
                g.memset(eps[:, :], 1e-5).then_inc(constants, 1)
                g.memset(vo[:, :, :, D:VW], 1.0).then_inc(constants, 1)
                pool.sem_inc(armed, 1)
                with pool.Fori(0, B // 2) as w:
                    for half in range(2):
                        t = Turn(w, half)
                        for a in range(2):
                            pool.wait_ge(part_lo.sem, part_lo.before(t, a + 1))
                            pool.wait_ge(part_hi.sem, part_hi.at(t, a + 1))
                            g.tensor_tensor(rem[:, a, :, :], qk[:, a, :, :], parts[:, a, 0, :, :],
                                            ALU.subtract).then_inc(rem_hi.sem, 1)
                        for a in range(2):
                            pool.wait_ge(rem_hi.sem, rem_hi.at(t, a + 1))
                            pool.wait_ge(part_mid.sem, part_mid.at(t, a + 1))
                            g.tensor_tensor(rem[:, a, :, :], rem[:, a, :, :], parts[:, a, 1, :, :],
                                            ALU.subtract).then_inc(rem_mid.sem, 1)

            @block.scalar
            def _(act):
                s = nc.scalar
                act.wait_ge(armed, 1)
                act.wait_ge(constants, 2)
                with act.Fori(0, B // 2) as w:
                    for half in range(2):
                        t = Turn(w, half)
                        act.wait_ge(var_ready.sem, var_ready.at(t))
                        s.activation(std[:, :], mv[:, :, 1], ACT.Sqrt, bias=eps[:, 0:1]).then_inc(std_ready.sem, 1)
                        act.wait_ge(stored["xt"].sem, stored["xt"].before(t))
                        R.wait_full(act, t, "x0")
                        R.released("x0", s.activation(xT[:, half, 0, :], R.bank("x0")[:, :], ACT.Copy))
                        act.wait_ge(stored["qf"].sem, stored["qf"].before(t))
                        act.wait_ge(stored["parts"].sem, stored["parts"].before(t))
                        for a, name in ((0, "q"), (1, "k")):
                            for h in range(2):
                                job = f"{name}{h}"
                                R.wait_full(act, t, job)
                                R.released(job, s.activation(qk[:, a, h, :], R.bank(job)[:, :],
                                                             ACT.Copy, scale=0.25 if a == 0 else 1.0))
                            for h in range(2):
                                R.wait_read(act, t, f"{name}{h}")
                            s.activation(parts[:, a, 0, :, :], qk[:, a, :, :], ACT.Copy).then_inc(part_hi.sem, 1)
                        for a in range(2):
                            act.wait_ge(rem_hi.sem, rem_hi.at(t, a + 1))
                            s.activation(parts[:, a, 1, :, :], rem[:, a, :, :], ACT.Copy).then_inc(part_mid.sem, 1)
                        for h in range(2):
                            R.wait_full(act, t, f"w{h}")
                            R.released(f"w{h}", s.activation(vT[:, h, :], R.bank(f"w{h}")[:, :], ACT.Copy))
                        for a in range(2):
                            act.wait_ge(rem_mid.sem, rem_mid.at(t, a + 1))
                            s.activation(parts[:, a, 2, :, :], rem[:, a, :, :], ACT.Copy).then_inc(part_lo.sem, 1)
                        act.wait_ge(gate_in.sem, gate_in.at(t))
                        s.activation(gl[:, :, :], gl[:, :, :], ACT.Exp).then_inc(gate_exp.sem, 1)

            @block.vector
            def _(dve):
                v = nc.vector
                dve.wait_ge(armed, 1)
                dve.wait_ge(constants, 2)
                ch = Chain(dve, dve_chain, 6)
                with dve.Fori(0, B // 2) as w:
                    for half in range(2):
                        t = Turn(w, half)
                        ch.start(t)
                        dve.wait_ge(x_in[half], w * 16 + 16)
                        for i in range(TT):
                            last = v.bn_stats(stats[:, i, :], xin[:, half, i, :])
                        ch.link(last)
                        v.memset(pad[:, 0:1], 0.0)
                        for i in range(TT):
                            last = v.bn_aggr(mv[:, i, :], stats[:, i, :])
                        last.then_inc(var_ready.sem, 1)
                        dve.wait_ge(std_ready.sem, std_ready.at(t))
                        ch.link(v.reciprocal(rstd[:, :], std[:, :]))
                        for i in range(TT):
                            last = v.tensor_scalar(xn[:, i, :], xin[:, half, i, :], mv[:, i, 0:1], rstd[:, i:i + 1],
                                                   ALU.subtract, ALU.mult)
                            last.then_inc(xn_ready.sem, 1)
                        R.wait_full(dve, t, "x1")
                        R.released("x1", v.tensor_copy(xT[:, half, 1, :], R.bank("x1")[:, :]))
                        dve.wait_ge(stored["v"].sem, stored["v"].before(t))
                        for j in range(2):
                            R.wait_full(dve, t, f"v{j}")
                            for i in range(2):
                                v.tensor_copy(vo[:, 2 * j + i, :, 0:D],
                                              R.bank(f"v{j}")[:, i * C:i * C + C].rearrange("p (h d) -> p h d", h=H))
                            last = v.tensor_copy(vn[:, 2 * j:2 * j + 2, :], R.bank(f"v{j}")[:, :].rearrange("p (i n) -> p i n", i=2))
                            R.released(f"v{j}", last)
                        R.wait_full(dve, t, "kv")
                        dve.wait_ge(stored["kc"].sem, stored["kc"].before(t))
                        kv = R.bank("kv")
                        for h in range(2):
                            v.tensor_tensor(kcs[:, h, :, :], kv[:, None, NB * h:NB * h + NB].broadcast_to([P, 8, NB]),
                                            head_rows[:, :, None].broadcast_to([P, 8, NB]), ALU.mult)\
                             .then_inc(kc_ready.sem, 1)
                            last = v.tensor_copy(vcr[:, h, :, :], kv[:, None, NB * (2 + h):NB * (3 + h)]
                                                 .broadcast_to([P, HG, NB]))
                        R.released("kv", last)
                        R.wait_full(dve, t, "gt")
                        dve.wait_ge(stored["gt"].sem, stored["gt"].before(t))
                        R.released("gt", v.tensor_tensor(
                            gl[:, :, :], R.bank("gt")[:, 0:16].rearrange("p (i n) -> p i n", i=TT)[:, :, 0:3],
                            bgb[:, None, :].broadcast_to([P, TT, 3]), ALU.add))
                        R.wait_read(dve, t, "gt")
                        ch.link(v.tensor_reduce(gm[:, :], gl[:, :, :], AX.X, ALU.max))
                        v.tensor_tensor(gl[:, :, :], gl[:, :, :], gm[:, :, None].broadcast_to([P, TT, 3]),
                                        ALU.subtract).then_inc(gate_in.sem, 1)
                        dve.wait_ge(stored["vc"].sem, stored["vc"].before(t))
                        R.wait_full(dve, t, "vc")
                        for h in range(2):
                            last = v.tensor_tensor(
                                vcs[:, h, :, :, :], R.bank("vc")[:, P * h:P * h + P].rearrange("p (g h d) -> p g h d", g=2, h=HG),
                                quad_rows[:, None, :, None].broadcast_to([P, 2, HG, D]), ALU.mult)
                        R.released("vc", last)
                        dve.wait_ge(gate_exp.sem, gate_exp.at(t))
                        ch.link(v.tensor_reduce(gs[:, :], gl[:, :, :], AX.X, ALU.add))
                        ch.link(v.reciprocal(gm[:, :], gs[:, :]))
                        ch.link(v.tensor_tensor(gl[:, :, :], gl[:, :, :], gm[:, :, None].broadcast_to([P, TT, 3]), ALU.mult))
                        v.tensor_tensor(gl[:, :, 0], gl[:, :, 0], any_ok[:, :], ALU.mult).then_inc(gate_ready.sem, 1)
                        ch.end()

            @block.tensor
            def _(pe):
                mm, tr = nc.tensor.matmul, nc.tensor.transpose
                pe.wait_ge(armed, 1)
                with pe.Fori(0, B // 2) as w:
                    for half in range(2):
                        t = Turn(w, half)
                        for c in range(2):
                            R.wait_free(pe, t, f"x{c}")
                            for i in range(TT):
                                if c == 0:
                                    pe.wait_ge(xn_ready.sem, xn_ready.at(t, i + 1))
                                last = tr(R.bank(f"x{c}")[:, i * P:i * P + P], xn[:, i, c * P:c * P + P], ident[:, :])
                            R.filled(f"x{c}", last)
                        for c in range(2):
                            R.wait_read(pe, t, f"x{c}")
                        for name, wt in (("q", wq), ("k", wk)):
                            for h in range(2):
                                job = f"{name}{h}"
                                R.wait_free(pe, t, job)
                                for c in range(2):
                                    last = mm(R.bank(job)[:, :], wt[:, c, h * P:h * P + P], xT[:, half, c, :],
                                              start=(c == 0), stop=(c == 1))
                                R.filled(job, last)
                        for j in range(2):
                            R.wait_free(pe, t, f"v{j}")
                            for i in range(2):
                                for c in range(2):
                                    last = mm(R.bank(f"v{j}")[:, i * C:i * C + C], xT[:, half, c, (2 * j + i) * P:(2 * j + i + 1) * P],
                                              wv[:, c, :], start=(c == 0), stop=(c == 1))
                            R.filled(f"v{j}", last)
                        for j in range(2):
                            R.wait_read(pe, t, f"v{j}")
                        for h in range(2):
                            R.wait_free(pe, t, f"w{h}")
                            for i in range(TT):
                                last = tr(R.bank(f"w{h}")[:, i * P:i * P + P], vn[:, i, P * h:P * h + P], ident[:, :])
                            R.filled(f"w{h}", last)
                        R.wait_free(pe, t, "kv")
                        for kind in range(2):
                            for h in range(2):
                                R.wait_read(pe, t, f"{'kw'[kind]}{h}")
                        for kind in range(2):
                            for h in range(2):
                                src = (qk[:, 1, h, :] if kind == 0 else vT[:, h, :]).rearrange("p (n j) -> p n j", j=BLK)
                                o = NB * (2 * kind + h)
                                for j in range(BLK):
                                    last = mm(R.bank("kv")[:, o:o + NB], (wck, wcv)[kind][:, j, :], src[:, :, j],
                                              start=(j == 0), stop=(j == BLK - 1))
                        R.filled("kv", last)
                        R.wait_free(pe, t, "gt")
                        for i in range(TT):
                            for c in range(2):
                                last = mm(R.bank("gt")[:, 4 * i:4 * i + 3], xT[:, half, c, i * P:i * P + P], wgate[:, c, :],
                                          start=(c == 0), stop=(c == 1))
                        R.filled("gt", last)
                        R.wait_free(pe, t, "vc")
                        R.wait_read(pe, t, "kv")
                        for h in range(2):
                            last = mm(R.bank("vc")[:, P * h:P * h + P], vcr[:, h, :, :].rearrange("p r n -> p (r n)"),
                                      ident[:, :], start=True, stop=True)
                        R.filled("vc", last)
        projecting.close()

        inner = ExitStack()
        with inner:
            sb, ps, sem = make(inner)
            SP3 = 96
            qo = sb("qo", [SP3, 2, HG, T], BF16)
            ko = sb("ko", [SP3, 2, HG, T], BF16)
            qf = sb("qf2", [64, 2, T])
            kc = sb("kc", [64, 2, P])
            vc = sb("vc", [P, 2, HG * D])
            vv = sb("vv", [P, 2, TT, HG, VW])
            gt = sb("gt", [P, 2, TT, 3])
            xt = sb("xt", [P, 2, 2, P])
            lc = sb("lc", [P, TT, HG, NB + 4])
            top = sb("top", [P, TT, HG, 8])
            strike = sb("strike", [P, TT, HG, 8])
            struck = sb("struck", [P, TT, HG, NB + 4])
            pc = sb("pc", [P, TT, HG, NB])
            csum = sb("csum", [P, TT * HG])
            cfac = sb("cfac", [P, TT, HG])
            pcT = sb("pcT", [P, T])
            co = sb("co", [P, TT, HG * D])
            unsel = sb("unsel", [P, TT, HG, NB], BF16)
            bmax = sb("bmax", [P, TT, HG, NB])
            bsel = sb("bsel", [P, TT, HG, NB])
            smax = sb("smax", [P, TT * HG])
            smax_hi = sb("smax_hi", [P, TT * HG], BF16)
            lmax = sb("lmax", [P, HG * TT])
            shift_s = sb("shift_s", [P, TT, HG, NB], BF16)
            shift_l = sb("shift_l", [P, TT, HG, NB], BF16)
            shiftT = sb("shiftT", [P, 2, T], BF16)
            OFFS = [0, 512, 896, 1152]
            pts = sb("pts", [P, 2, 1280])
            ptl = sb("ptl", [P, 2, T])
            pto = sb("pto", [P, HG, TT - 1, 32])
            rs = sb("rs", [P, 4 * TT])
            fs = sb("fs", [P, 4 * TT])
            on = sb("on", [P, 2, 4 * TT, D])
            at = sb("at", [P, TT, HG, D])
            th = sb("th", [P, 2, 512])
            gs = sb("gs2", [P, 2, 512])
            hT = sb("hT", [P, FT, P])
            sim = sb("sim", [P, 2, PH, KEYS])
            t8 = sb("t8", [P, 2, PH, 8])
            marks = sb("marks", [P, 2, PH, KEYS])
            xy = sb("xy", [P, 2, PH, KEYS])
            cand = sb("cand", [P, PH, 8, 8])
            c8 = sb("c8", [P, PH, 8])
            e8 = sb("e8", [P, PH, 8])
            esum = sb("esum", [P, PH])
            erec = sb("erec", [P, PH])
            nmax = sb("nmax", [P, PH])
            sumxy = sb("sumxy", [P, PH, XK, KEYS])
            ex = sb("ex", [P, 2, EX])
            mw = sb("mw", [P, 2, EX])
            cw = sb("cw", [P, EX])
            csm = sb("csm", [P, 1])
            clast = sb("clast", [P, 1])
            tw = sb("tw", [P, 2, 512])
            sw = sb("sw", [P, EX])
            cwT = sb("cwT", [P, EX // P, P])
            yo = sb("yo", [P, C])

            q_jobs = ["lc"] + [f"p{h}{k}" for h in range(HG) for k in (3, 0, 1)] + ["m0", "m1"]
            k_jobs = ["aug", "pcT", "off", "co"]
            for h in range(HG):
                k_jobs += [f"s{h}0", f"s{h}1", f"s{h}2", f"d{h}"]

            def ring(name, n, jobs, front=()):
                return Banks([ps(f"{name}_bank{i}", [P, 512]) for i in range(n)],
                             [sem(f"{name}_full{i}") for i in range(n)],
                             [sem(f"{name}_read{i}") for i in range(n)], jobs, front)
            Q = ring("q", 2, q_jobs, front=q_jobs)
            K = ring("k", 2, k_jobs)
            F = ring("f", 2, ["w0", "w1", "sim", "g0", "u0", "g1", "u1", "t0", "t1"], front=["sim"])
            O = ring("o", 1, ["o0", "o1"])
            Y = ring("y", 1, ["y"])
            near_in = [sem("near_in0"), sem("near_in1")]
            parts_in = [sem("parts_in0"), sem("parts_in1")]
            late_in = [sem("late_in0"), sem("late_in1")]
            N_NEAR, N_PARTS, N_LATE = 3, 9, 3
            S = {}
            for name, per, ahead in (
                    ("lc_done", 1, 0), ("top_done", 1, 0), ("strike_done", 1, 0),
                    ("pc_in", 1, 0), ("pc_exp", 1, 0), ("cfac_done", 1, 0), ("pc_done", 1, 0),
                    ("smax_done", 1, 0), ("shift_lo", 1, 0), ("shift_done", 1, 0),
                    ("pv", HG, 1), ("at_sum", 2, 0), ("at_done", 1, 1),
                    ("th_done", 2, 0), ("t8_done", 1, 0), ("xy_in", 1, 0), ("xy_done", 1, 0), ("cand_done", 1, 0),
                    ("c8_done", 1, 0), ("e8_in", 1, 0), ("e8_exp", 1, 0), ("nmax_done", 1, 0), ("sum_done", PH, 0),
                    ("ex_done", PH, 0), ("mw_done", PH, 0), ("cw_sum", PH - 1, 0), ("clast_done", 1, 0),
                    ("cw_done", 1, 0), ("tw_done", 2, 0), ("st_at", 16, 1), ("st_y", 16, 1)):
                S[name] = Signal(sem(name), per, ahead=bool(ahead))
            armed = sem("armed_u")
            near_chain, far_chain = sem("near_chain"), sem("far_chain")
            constants = sem("constants_u")

            def need(eng, name, t, n=None):
                eng.wait_ge(S[name].sem, S[name].at(t, n))

            def need_before(eng, name, t, n=None):
                eng.wait_ge(S[name].sem, S[name].before(t, n))

            def done(name, ins):
                ins.then_inc(S[name].sem, 1)

            def steps(eng, step, lead=None):
                if lead:
                    lead(Turn(0, 0, step=None))
                with eng.Fori(0, UNITS // 2 - 1) as w:
                    step(Turn(w, 0))
                    step(Turn(w, 1))
                step(Turn(UNITS // 2 - 1, 0))
                step(Turn(UNITS // 2 - 1, 1, tail=True))

            def loaded_by(eng, lot, n, t):
                eng.wait_ge(lot[t.half], t.pair * (16 * n) + 16 * n)

            block = inner.enter_context(nc.Block())

            @block.sync
            def _(sp):
                qs = s_qs.rearrange("b (g h) r d t -> (b g) r d h t", g=G)
                ks = s_ks.rearrange("b (g h) r d t -> (b g) (r d) h t", g=G)
                qff = s_qf.rearrange("b g p t -> (b g) p t")
                kcf = s_kc.rearrange("b g p n -> (b g) p n")
                vcf = s_vc.rearrange("b g p n -> (b g) p n")
                vf = s_v.rearrange("b i p (g n) -> b g p i n", g=G)

                def send(pairs, to, n):
                    assert len(pairs) == n
                    for dst, src in pairs:
                        sp.dma_start(dst, src).then_inc(to, 16)

                def load_near(b, g, u, half):
                    send([(qf[:, half, :], row(qff, u)), (kc[:, half, :], row(kcf, u)),
                          (xt[:, half, :, :], row(s_xt, b)[:, :, g * P:g * P + P])], near_in[half], N_NEAR)

                def load_parts(u, half):
                    send([(qo[16 * n:16 * n + 16, half, :, :], row(qs, u)[r]) for n, r in enumerate((0, 0, 0, 1, 1, 2))]
                         + [(ko[at_row:at_row + 16 * n, half, :, :], row(ks, u)[0:16 * n])
                            for at_row, n in ((0, 3), (48, 2), (80, 1))], parts_in[half], N_PARTS)

                def load_late(b, g, u, half):
                    send([(vc[:, half, :], row(vcf, u)),
                          (vv[:, half, :, :, :].rearrange("p i h d -> p i (h d)"), row(vf, b)[g]),
                          (gt[:, half, :, :].rearrange("p i n -> p (i n)"), row(s_gt, b))], late_in[half], N_LATE)

                for u in range(2):
                    load_near(0, u, u, u)
                    load_parts(u, u)
                    load_late(0, u, u, u)
                sp.wait_ge(armed, 1)

                def step(t, b, g, load_next=True):
                    half, u = t.half, t.index + 2
                    if load_next:
                        F.wait_full(sp, t, "u1")
                        load_near(b, g, u, half)
                        K.wait_full(sp, t, "d3")
                        load_parts(u, half)
                        O.wait_read(sp, t, "o1")
                        load_late(b, g, u, half)
                    need(sp, "at_done", t)
                    sp.dma_start(row(s_o, t.index).rearrange("i p n -> p i n"),
                                 at[:, :, :, :].rearrange("p i h d -> p i (h d)")).then_inc(S["st_at"].sem, 16)
                    Y.wait_read(sp, t, "y")
                    sp.dma_start(row(s_y, t.index), yo[:, :]).then_inc(S["st_y"].sem, 16)

                def four(b, last=False):
                    for g in range(G):
                        t = Turn(b * 2 + g // 2, g % 2, tail=last and g == G - 1)
                        step(t, b if g < 2 else b + 1, (g + 2) % G, load_next=not last or g < 2)

                with sp.Fori(0, B - 1) as b:
                    four(b)
                four(B - 1, last=True)
                for n in ("st_at", "st_y"):
                    sp.wait_ge(S[n].sem, 16 * (UNITS + 1))

            @block.gpsimd
            def _(pool):
                g_ = nc.gpsimd
                for s in S.values():
                    if s.ahead:
                        pool.sem_inc(s.sem, s.per)
                for r in (Q, K, F, O, Y):
                    for s in r.free:
                        pool.sem_inc(s, 1)
                for m, val in ((lc[:, :, :, NB:NB + 4], LOWEST), (strike[:, :, :, 4:8], LOWEST), (bmax[:, :, :, :], 0.0),
                               (shift_l[:, :, :, 2:NB], 0.0), (pto[:, :, :, :], 0.0), (pad[:, 0:4], 0.0)):
                    g_.memset(m, val).then_inc(constants, 1)
                pool.sem_inc(armed, 1)
                pool.wait_ge(constants, 6)

                def pad_wait():
                    g_.tensor_tensor(pad[:, 2:3], pad[:, 3:4], pad[:, 3:4], ALU.add)

                def compressed(t):
                    Q.wait_read(pool, t, "lc")
                    done("lc_done", g_.tensor_tensor(lc[:, :, :, 0:NB], lc[:, :, :, 0:NB],
                                                     block_no[:, :, None, :].broadcast_to([P, TT, HG, NB]), ALU.add))

                def shifts(t):
                    need(pool, "top_done", t)
                    pad_wait()
                    done("strike_done", g_.tensor_copy(strike[:, :, :, 0:4], top[:, :, :, 0:4]))
                    done("pc_in", g_.tensor_tensor(pc[:, :, :, :], lc[:, :, :, 0:NB],
                                                   top[:, :, :, 0:1].broadcast_to([P, TT, HG, NB]), ALU.subtract))
                    need(pool, "smax_done", t)
                    done("shift_lo", g_.tensor_tensor(
                        shift_s[:, :, :, 0:NB - 1], unsel[:, :, :, 0:NB - 1],
                        smax_hi[:, :].rearrange("p (i h) -> p i h", i=TT)[:, :, :, None].broadcast_to([P, TT, HG, NB - 1]),
                        ALU.add))
                    need(pool, "cfac_done", t)
                    done("pc_done", g_.tensor_tensor(pc[:, :, :, :], pc[:, :, :, :],
                                                     cfac[:, :, :, None].broadcast_to([P, TT, HG, NB]), ALU.mult))

                def candidates(t, behind=None):
                    need(pool, "xy_in", t)
                    done("xy_done", g_.tensor_tensor(xy[:, :, :, :], xy[:, :, :, :], sim[:, :, :, :], ALU.add))
                    done("cand_done", g_.tensor_tensor(cand[:, :, :, :], t8[:, 0, :, :, None].broadcast_to([P, PH, 8, 8]),
                                                       t8[:, 1, :, None, :].broadcast_to([P, PH, 8, 8]), ALU.add))
                    need(pool, "xy_done", t)
                    for h in range(PH):
                        done("sum_done", g_.tensor_tensor(sumxy[:, h, :, :], xy[:, 0, h, 0:XK, None].broadcast_to([P, XK, KEYS]),
                                                          xy[:, 1, h, None, :].broadcast_to([P, XK, KEYS]), ALU.add))
                        if h == 0:
                            need(pool, "c8_done", t)
                            done("e8_in", g_.tensor_tensor(e8[:, :, :], c8[:, :, :], c8[:, :, 0:1].broadcast_to([P, PH, 8]),
                                                           ALU.subtract))
                            if behind:
                                silu_weights(behind)

                def weights(t):
                    for h in range(1, PH):
                        need(pool, "mw_done", t, h + 1)
                        if h > 1:
                            need(pool, "cw_sum", t, h - 1)
                        done("cw_sum", g_.tensor_tensor(cw[:, :], cw[:, :], mw[:, h % 2, :], ALU.add))

                def silu_weights(t):
                    need(pool, "clast_done", t)
                    F.wait_read(pool, t, "w0")
                    F.wait_read(pool, t, "w1")
                    done("cw_done", g_.tensor_tensor(cw[:, :], cw[:, :], sw[:, :], ALU.mult))

                def branches(t, hp):
                    if hp == 0:
                        need_before(pool, "st_at", t)
                    O.wait_read(pool, t, f"o{hp}")
                    k0, k1 = (on[:, hp, 2 * TT * k:2 * TT * (k + 1), :].rearrange("p (h i) d -> p i h d", h=2)
                              for k in range(2))
                    done("at_sum", g_.tensor_tensor(at[:, :, 2 * hp:2 * hp + 2, :], k0, k1, ALU.add))
                    if hp == 0:
                        return
                    need(pool, "at_sum", t)
                    K.wait_read(pool, t, "co")
                    done("at_done", g_.tensor_tensor(at[:, :, :, :].rearrange("p i h d -> p i (h d)"),
                                                     at[:, :, :, :].rearrange("p i h d -> p i (h d)"), co[:, :, :], ALU.add))

                def lead(n):
                    compressed(n)
                    candidates(n)
                    shifts(n)

                def step(t):
                    n = None if t.tail else t.next()
                    weights(t)
                    if n:
                        compressed(n)
                    if n:
                        candidates(n, behind=t)
                    else:
                        silu_weights(t)
                    branches(t, 0)
                    if n:
                        shifts(n)
                    branches(t, 1)
                steps(pool, step, lead)

            @block.scalar
            def _(act):
                s = nc.scalar
                act.wait_ge(armed, 1)
                act.wait_ge(constants, 6)

                def head(t, h):
                    slot = h % 2
                    if h < 2:
                        need_before(act, "pv", t, h + 3)
                    else:
                        need(act, "pv", t, h - 1)
                    for j in range(3):
                        K.wait_full(act, t, f"s{h}{j}")
                        bank = K.bank(f"s{h}{j}")
                        n = T - j * P
                        last = s.activation(pts[:, slot, OFFS[j]:OFFS[j] + n], bank[:, 0:n], ACT.Exp)
                        if j == 1:
                            last = s.activation(pts[0:112, slot, OFFS[3]:OFFS[3] + P], bank[0:112, n:n + P], ACT.Exp)
                        K.released(f"s{h}{j}", last)
                    K.wait_full(act, t, f"d{h}")
                    K.released(f"d{h}", s.activation(ptl[:, slot, :], K.bank(f"d{h}")[:, :], ACT.Exp))

                def expert(t, h):
                    need(act, "nmax_done", t)
                    need(act, "sum_done", t, h + 1)
                    if h >= 2:
                        need(act, "mw_done", t, h - 1)
                    done("ex_done", s.activation(ex[:, h % 2, :], sumxy[:, h, :, :].rearrange("p a b -> p (a b)"),
                                                 ACT.Exp, bias=nmax[:, h:h + 1]))

                def tanh(t, job, dst, name):
                    F.wait_full(act, t, job)
                    done(name, s.activation(dst, F.bank(job)[:, :], ACT.Tanh, scale=0.5))

                def key_scores(n):
                    F.wait_full(act, n, "sim")
                    F.released("sim", s.activation(sim[:, :, :, :].rearrange("p a h k -> p (a h k)"),
                                                   F.bank("sim")[:, :], ACT.Copy))

                def e8_exp(n):
                    need(act, "e8_in", n)
                    done("e8_exp", s.activation(e8[:, :, :], e8[:, :, :], ACT.Exp))

                def pc_exp(n):
                    need(act, "pc_in", n)
                    done("pc_exp", s.activation(pc[:, :, :, :], pc[:, :, :, :], ACT.Exp))

                def shifts(t):
                    K.wait_full(act, t, "aug")
                    K.released("aug", s.activation(shiftT[:, :, :].rearrange("p a t -> p (a t)"),
                                                   K.bank("aug")[:, :].bitcast(BF16), ACT.Copy))

                def openings(t):
                    K.wait_full(act, t, "pcT")
                    K.released("pcT", s.activation(pcT[:, :], K.bank("pcT")[:, :], ACT.Copy))
                    expert(t, 2)
                    need_before(act, "pv", t)
                    K.wait_full(act, t, "off")
                    K.released("off", s.activation(pto[96:128, :, :, :].rearrange("p h i c -> p (h i c)"),
                                                   K.bank("off")[96:128, 0:384], ACT.Exp))
                    tanh(t, "g0", th[:, 0, :], "th_done")
                    need_before(act, "at_done", t)
                    K.wait_full(act, t, "co")
                    K.released("co", s.activation(co[:, :, :].rearrange("p i n -> p (i n)"),
                                                  K.bank("co")[:, 0:TT * HG * D], ACT.Copy))
                    expert(t, 3)

                def lead(n):
                    key_scores(n)
                    e8_exp(n)
                    pc_exp(n)

                def step(t):
                    n = None if t.tail else t.next()
                    tanh(t, "w0", tw[:, 0, :], "tw_done")
                    expert(t, 0)
                    tanh(t, "w1", tw[:, 1, :], "tw_done")
                    expert(t, 1)
                    shifts(t)
                    if n:
                        key_scores(n)
                    openings(t)
                    head(t, 0)
                    head(t, 1)
                    tanh(t, "g1", th[:, 1, :], "th_done")
                    head(t, 2)
                    if n:
                        e8_exp(n)
                    head(t, 3)
                    for j in range(2):
                        F.wait_full(act, t, f"t{j}")
                        F.released(f"t{j}", s.activation(cwT[:, 4 * j:4 * j + 4, :].rearrange("p e t -> p (e t)"),
                                                         F.bank(f"t{j}")[:, :], ACT.Copy))
                    if n:
                        pc_exp(n)
                steps(act, step, lead)

            @block.vector
            def _(dve):
                v = nc.vector
                dve.wait_ge(armed, 1)
                dve.wait_ge(constants, 6)
                cn = Chain(dve, near_chain, 10)
                cf = Chain(dve, far_chain, 10)

                def pad_wait():
                    v.memset(pad[:, 0:1], 0.0)

                def gate(t, j):
                    need(dve, "th_done", t, j + 1)
                    F.released(f"g{j}", v.scalar_tensor_tensor(gs[:, j, :], th[:, j, :], 1.0, F.bank(f"g{j}")[:, :],
                                                               ALU.add, ALU.mult))

                def up(t, j):
                    F.wait_read(dve, t, f"g{j}")
                    F.wait_full(dve, t, f"u{j}")
                    F.released(f"u{j}", v.tensor_tensor(hT[:, 4 * j:4 * j + 4, :].rearrange("p f t -> p (f t)"), gs[:, j, :],
                                                        F.bank(f"u{j}")[:, :], ALU.mult))

                def block_max(t, h, part):
                    job, tiles = ((f"p{h}3", ((3, 0),)), (f"p{h}0", ((0, 0), (2, P))), (f"p{h}1", ((1, 0),)))[part]
                    Q.wait_full(dve, t, job)
                    for i, o in tiles:
                        n = 8 * (i + 1)
                        last = v.tensor_reduce(bmax[:, i, h, 0:n],
                                               Q.bank(job)[:, o:o + n * BLK].rearrange("p (n j) -> p n j", j=BLK),
                                               AX.X, ALU.max)
                    Q.released(job, last)

                def compressed(t):
                    Q.wait_full(dve, t, "lc")
                    Q.released("lc", v.tensor_tensor(
                        lc[:, :, :, 0:NB], Q.bank("lc")[:, :].rearrange("p (i h n) -> p i h n", i=TT, h=HG),
                        block_ok[:, :, None, :].broadcast_to([P, TT, HG, NB]), ALU.mult))

                def best_blocks(t):
                    need(dve, "lc_done", t)
                    pad_wait()
                    for i in range(TT):
                        for h in range(HG):
                            last = v.max(top[:, i, h, :], lc[:, i, h, 0:NB])
                    done("top_done", last)

                def local_max(t):
                    for j in range(2):
                        Q.wait_full(dve, t, f"m{j}")
                        last = v.tensor_reduce(lmax[:, 8 * j:8 * j + 8], Q.bank(f"m{j}")[:, :].rearrange(
                            "p (n k) -> p n k", k=64), AX.X, ALU.max, negate=True)
                        Q.released(f"m{j}", last)

                def shifts(t):
                    ch = cn
                    need(dve, "strike_done", t)
                    pad_wait()
                    for i in range(TT):
                        for h in range(HG):
                            last = v.match_replace(struck[:, i, h, :], strike[:, i, h, :], lc[:, i, h, :], TAKEN)
                    ch.link(last)
                    ch.link(v.tensor_scalar(unsel[:, :, :, :], struck[:, :, :, 0:NB], TAKEN / 10, NEG, ALU.is_lt, ALU.mult))
                    ch.link(v.tensor_tensor(bsel[:, :, :, :], bmax[:, :, :, :], unsel[:, :, :, :], ALU.add))
                    ch.link(v.tensor_reduce(smax[:, :], bsel[:, :, :, :].rearrange("p i h n -> p (i h) n"), AX.X,
                                            ALU.max, negate=True))
                    done("smax_done", v.tensor_copy(smax_hi[:, :], smax[:, :]))
                    need(dve, "smax_done", t)
                    v.tensor_tensor(shift_s[:, :, :, NB - 1], smax[:, :].rearrange("p (i h) -> p i h", i=TT),
                                    smax_hi[:, :].rearrange("p (i h) -> p i h", i=TT), ALU.subtract)
                    lm = lmax[:, :].rearrange("p (h i) -> p i h", h=HG)
                    ch.link(v.tensor_copy(shift_l[:, :, :, 0], lm))
                    done("shift_done", v.tensor_tensor(shift_l[:, :, :, 1], lm, shift_l[:, :, :, 0], ALU.subtract))
                    need(dve, "pc_exp", t)
                    loaded_by(dve, late_in, N_LATE, t)
                    ch.link(v.tensor_reduce(csum[:, :], pc[:, :, :, :].rearrange("p i h n -> p (i h) n"), AX.X, ALU.add))
                    ch.link(v.reciprocal(csum[:, :], csum[:, :]))
                    done("cfac_done", v.tensor_tensor(cfac[:, :, :], csum[:, :].rearrange("p (i h) -> p i h", i=TT),
                                                      gt[:, t.half, :, 0:1].broadcast_to([P, TT, HG]), ALU.mult))

                def best_keys(t):
                    ch = cn
                    F.wait_read(dve, t, "sim")
                    pad_wait()
                    for a in range(2):
                        for h in range(PH):
                            last = v.max(t8[:, a, h, :], sim[:, a, h, :])
                    done("t8_done", last)
                    need(dve, "t8_done", t)
                    pad_wait()
                    for a in range(2):
                        for h in range(PH):
                            last = v.match_replace(marks[:, a, h, :], t8[:, a, h, :], sim[:, a, h, :], TAKEN)
                    ch.link(last)
                    done("xy_in", v.tensor_scalar(xy[:, :, :, :], marks[:, :, :, :], TAKEN / 10, NEG, ALU.is_lt, ALU.mult))

                def best_pairs(t):
                    ch = cn
                    need(dve, "cand_done", t)
                    pad_wait()
                    for h in range(PH):
                        last = v.max(c8[:, h, :], cand[:, h, :, :].rearrange("p a b -> p (a b)"))
                    done("c8_done", last)
                    need(dve, "c8_done", t)
                    done("nmax_done", v.tensor_scalar(nmax[:, :], c8[:, :, 0], -1.0, None, ALU.mult))

                def pair_sums(t):
                    ch = cn
                    need(dve, "e8_exp", t)
                    ch.link(v.tensor_reduce(esum[:, :], e8[:, :, :], AX.X, ALU.add))
                    ch.link(v.reciprocal(erec[:, :], esum[:, :]))

                def expert(t, h):
                    dst = cw[:, :] if h == 0 else mw[:, h % 2, :]
                    need(dve, "sum_done", t, h + 1)
                    if h == 3:
                        need(dve, "cw_sum", t, 1)
                    cf.link(v.tensor_scalar(dst, sumxy[:, h, :, :].rearrange("p a b -> p (a b)"), c8[:, h, 7:8],
                                            erec[:, h:h + 1], ALU.is_ge, ALU.mult))
                    need(dve, "ex_done", t, h + 1)
                    done("mw_done", v.tensor_tensor(dst, dst, ex[:, h % 2, :], ALU.mult))

                def last_expert(t):
                    need(dve, "cw_sum", t)
                    cf.link(v.tensor_reduce(csm[:, :], cw[:, :], AX.X, ALU.add))
                    cf.link(v.tensor_tensor(clast[:, :], cw[:, EX - 1:EX], csm[:, :], ALU.subtract))
                    done("clast_done", v.tensor_scalar(cw[:, EX - 1:EX], clast[:, :], float(PH), None, ALU.add))

                def expert_silu(t, j):
                    need(dve, "tw_done", t, j + 1)
                    F.released(f"w{j}", v.scalar_tensor_tensor(sw[:, 512 * j:512 * j + 512], tw[:, j, :], 1.0,
                                                               F.bank(f"w{j}")[:, :], ALU.add, ALU.mult))

                def normalize(t, hp):
                    need(dve, "pv", t, 2 * hp + 2)
                    bank = O.bank(f"o{hp}")[:, 0:4 * TT * VW].rearrange("p (n d) -> p n d", d=VW)
                    cf.link(v.reciprocal(rs[:, :], bank[:, :, D]))
                    cf.link(v.tensor_tensor(fs[:, :].rearrange("p (k h i) -> p k h i", k=2, h=2),
                                            rs[:, :].rearrange("p (k h i) -> p k h i", k=2, h=2),
                                            gt[:, t.half, :, 1:3].rearrange("p i k -> p k i")[:, :, None, :]
                                            .broadcast_to([P, 2, 2, TT]), ALU.mult))
                    if hp == 0:
                        need_before(dve, "at_done", t)
                    O.released(f"o{hp}", v.tensor_tensor(on[:, hp, :, :], bank[:, :, 0:D],
                                                         fs[:, :, None].broadcast_to([P, 4 * TT, D]), ALU.mult))

                def result(t):
                    Y.wait_full(dve, t, "y")
                    need_before(dve, "st_y", t)
                    Y.released("y", v.scalar_tensor_tensor(yo[:, :], Y.bank("y")[:, 0:C], 0.5, bdb[:, :],
                                                           ALU.mult, ALU.add))

                def lead(n):
                    cn.start(n)
                    compressed(n)
                    for h in range(HG):
                        for part in range(3):
                            block_max(n, h, part)
                    best_keys(n)
                    best_pairs(n)
                    pair_sums(n)
                    best_blocks(n)
                    local_max(n)
                    shifts(n)
                    cn.end()

                def step(t):
                    n = None if t.tail else t.next()
                    cf.start(t)
                    expert_silu(t, 0)
                    expert(t, 0)
                    expert_silu(t, 1)
                    expert(t, 1)
                    if n:
                        cn.start(n)
                        compressed(n)
                    expert(t, 2)
                    gate(t, 0)
                    if n:
                        for part in range(3):
                            block_max(n, 0, part)
                    up(t, 0)
                    expert(t, 3)
                    if n:
                        for part in range(3):
                            block_max(n, 1, part)
                        best_keys(n)
                    gate(t, 1)
                    if n:
                        block_max(n, 2, 0)
                        block_max(n, 2, 1)
                    last_expert(t)
                    if n:
                        block_max(n, 2, 2)
                        best_pairs(n)
                    up(t, 1)
                    normalize(t, 0)
                    if n:
                        for part in range(3):
                            block_max(n, 3, part)
                        pair_sums(n)
                        best_blocks(n)
                        local_max(n)
                        shifts(n)
                        cn.end()
                    result(t)
                    normalize(t, 1)
                    cf.end()
                steps(dve, step, lead)

            @block.tensor
            def _(pe):
                mm, tr = nc.tensor.matmul, nc.tensor.transpose
                pe.wait_ge(armed, 1)
                pe.wait_ge(constants, 6)

                def up_rows(t, name, j, k):
                    w_, kind = (wfg, 0) if name == "g" else (wfu, 1)
                    if k == 0:
                        F.wait_free(pe, t, f"{name}{j}")
                    o = P * (4 * j + k)
                    dst = F.bank(f"{name}{j}")[:, k * P:k * P + P]
                    mm(dst, bias3[:, kind, o:o + P], onesb[0:3, :], start=True, stop=False)
                    for c in range(2):
                        last = mm(dst, w_[:, c, o:o + P], xt[:, t.half, c, :], start=False, stop=(c == 1))
                    if k == 3:
                        F.filled(f"{name}{j}", last)

                def token_rows(t, job, w_, o):
                    F.wait_free(pe, t, job)
                    for c in range(2):
                        last = mm(F.bank(job)[:, :], xt[:, t.half, c, :], w_[:, c, o:o + 512], start=(c == 0), stop=(c == 1))
                    F.filled(job, last)

                def queries(t, h, part):
                    job, tiles = ((f"p{h}3", ((3, 0),)), (f"p{h}0", ((0, 0), (2, P))), (f"p{h}1", ((1, 0),)))[part]
                    Q.wait_free(pe, t, job)
                    bank = Q.bank(job)
                    for i, o in tiles:
                        n = P * (i + 1)
                        last = mm(bank[:, o:o + n], qo[:, t.half, h, P * i:P * i + P], ko[:, t.half, h, 0:n],
                                  start=True, stop=(i > 0))
                        if i == 0:
                            last = mm(bank[:, 0:P], identb[:, :], causal_ts[:, :], start=False, stop=True)
                    Q.filled(job, last)

                def window(t, j):
                    job = f"m{j}"
                    Q.wait_free(pe, t, job)
                    bank = Q.bank(job)
                    mm(bank[:, :], identb[:, :], window_ts[:, None, :, :].broadcast_to([P, 2, TT, 64]),
                       start=True, stop=True)
                    for h2 in range(2):
                        h = 2 * j + h2
                        for i in range(TT):
                            for q in range(4):
                                s0 = P * i + 32 * q
                                o = 64 * (TT * h2 + i)
                                k_ = (ko[:, t.half, h, s0 - 32:s0 + 32] if s0 else
                                      ko[:, t.half, h, 0:32][:, None, :].broadcast_to([SP3, 2, 32]))
                                last = mm(bank[32 * q:32 * q + 32, o:o + 64], qo[:, t.half, h, s0:s0 + 32], k_,
                                          start=False, stop=True, skip_group_check=True)
                    Q.filled(job, last)

                def keys_rows(t, h, part):
                    if part < 3:
                        job = f"s{h}{part}"
                        K.wait_free(pe, t, job)
                        bank = K.bank(job)
                        for i, o in (((0, 0),), ((1, 0), (3, 384)), ((2, 0),))[part]:
                            n, m = T - P * i, (P if i < 3 else 112)
                            mm(bank[0:m, o:o + n], ko[:, t.half, h, P * i:P * i + m], qo[:, t.half, h, P * i:T],
                               start=True, stop=False)
                            if i == 0:
                                mm(bank[:, 0:64], identb[:, :], causal_st[:, :], start=False, stop=False)
                            last = mm(bank[0:m, o:o + n], onehot[:, h, P * i:P * i + m], shiftT[:, 0, P * i:T],
                                      start=False, stop=True)
                    else:
                        job = f"d{h}"
                        K.wait_free(pe, t, job)
                        bank = K.bank(job)
                        mm(bank[:, :], identb[:, :], window_st[:, None, :].broadcast_to([P, TT, P]), start=True, stop=False)
                        for i in range(TT):
                            mm(bank[:, P * i:P * i + P], ko[:, t.half, h, P * i:P * i + P],
                               qo[:, t.half, h, P * i:P * i + P], start=False, stop=False)
                        last = mm(bank[:, :], headones[:, h, :], shiftT[:, 1, :], start=False, stop=True)
                    K.filled(job, last)

                def values(t, h, part):
                    hp, h2 = divmod(h, 2)
                    slot = h % 2
                    bank = O.bank(f"o{hp}")
                    if part == 0:
                        if h2 == 0:
                            O.wait_free(pe, t, f"o{hp}")
                        for j in (1, 2):
                            K.wait_read(pe, t, f"s{h}{j}")
                    if part < 3:
                        for i in ((0, 1), (2,), (3,))[part]:
                            o = VW * (TT * h2 + i)
                            for j in range(i + 1):
                                m = P if j < 3 else 112
                                c = OFFS[j] + P * (i - j)
                                mm(bank[:, o:o + VW], pts[0:m, slot, c:c + P], vv[0:m, t.half, j, h, :],
                                   start=(j == 0), stop=(j == i))
                        return
                    K.wait_read(pe, t, f"d{h}")
                    if h == 0:
                        K.wait_read(pe, t, "off")
                    for i in range(TT):
                        o = VW * (2 * TT + TT * h2 + i)
                        last = mm(bank[:, o:o + VW], ptl[:, slot, P * i:P * i + P], vv[:, t.half, i, h, :],
                                  start=True, stop=True)
                        if i:
                            last = mm(bank[0:32, o:o + VW], pto[:, h, i - 1, :], vv[:, t.half, i - 1, h, :],
                                      start=False, stop=True, skip_group_check=True)
                    done("pv", last)

                def compressed(t):
                    Q.wait_free(pe, t, "lc")
                    loaded_by(pe, near_in, N_NEAR, t)
                    for i in range(TT):
                        last = mm(Q.bank("lc")[:, P * i:P * i + P], qf[:, t.half, P * i:P * i + P], kc[:, t.half, :],
                                  start=True, stop=True)
                    Q.filled("lc", last)

                def openings(t, part):
                    job = ("aug", "pcT", "off", "co")[part]
                    bank = K.bank(job)
                    if job == "aug":
                        need(pe, "shift_lo", t)
                        need(pe, "shift_done", t)
                        K.wait_free(pe, t, job)
                        for k, src in enumerate((shift_s, shift_l)):
                            for i in range(TT):
                                o = T * k + P * i
                                last = tr(bank[:, :].bitcast(BF16)[:, o:o + P],
                                          src[:, i, :, :].rearrange("p h n -> p (h n)"), identb[:, :])
                    elif job == "pcT":
                        need(pe, "pc_done", t)
                        K.wait_free(pe, t, job)
                        for i in range(TT):
                            last = tr(bank[:, P * i:P * i + P], pc[:, i, :, :].rearrange("p h n -> p (h n)"), ident[:, :])
                    elif job == "off":
                        K.wait_free(pe, t, job)
                        mm(bank[96:128, 0:384], identb[:, 96:128], window_off[:, None, :].broadcast_to([P, 12, 32]),
                           start=True, stop=True)
                        for h in range(HG):
                            for i in range(TT - 1):
                                o = 32 * ((TT - 1) * h + i)
                                tq = slice(P * (i + 1), P * (i + 1) + 32)
                                mm(bank[96:128, o:o + 32], ko[:, t.half, h, P * i + 96:P * i + P], qo[:, t.half, h, tq],
                                   start=False, stop=False, skip_group_check=True)
                                last = mm(bank[96:128, o:o + 32], headones[:, h, 0:32], shiftT[:, 1, tq], start=False,
                                          stop=True, skip_group_check=True)
                    else:
                        K.wait_free(pe, t, job)
                        loaded_by(pe, late_in, N_LATE, t)
                        for i in range(TT):
                            last = mm(bank[:, 64 * i:64 * i + 64], pcT[:, P * i:P * i + P], vc[:, t.half, :],
                                      start=True, stop=True)
                    K.filled(job, last)

                def mlp_down(t, part):
                    if part == 0:
                        Y.wait_free(pe, t, "y")
                        F.wait_read(pe, t, "u1")
                    for f in (2 * part, 2 * part + 1):
                        mm(Y.bank("y")[:, 0:C], hT[:, f, :], wfd[:, f, :], start=(f == 0), stop=False)

                def transposed_weights(t):
                    need(pe, "cw_done", t)
                    for j in range(2):
                        F.wait_free(pe, t, f"t{j}")
                        for e in range(4):
                            o = P * (4 * j + e)
                            last = tr(F.bank(f"t{j}")[:, P * e:P * e + P], cw[:, o:o + P], ident[:, :])
                        F.filled(f"t{j}", last)

                def experts_down(t, j):
                    F.wait_read(pe, t, f"t{j}")
                    for e in range(4 * j, 4 * j + 4):
                        last = mm(Y.bank("y")[:, 0:C], cwT[:, e, :], wup[:, e, :], start=False, stop=(e == 7))
                    if j == 1:
                        Y.filled("y", last)

                def lead(n):
                    compressed(n)
                    token_rows(n, "sim", wsim, 0)
                    loaded_by(pe, parts_in, N_PARTS, n)
                    for h in range(HG):
                        for part in range(3):
                            queries(n, h, part)
                    window(n, 0)
                    window(n, 1)

                def step(t):
                    n = None if t.tail else t.next()
                    token_rows(t, "w0", wdn, 0)
                    token_rows(t, "w1", wdn, 512)
                    if n:
                        compressed(n)
                    openings(t, 0)
                    if n:
                        token_rows(n, "sim", wsim, 0)
                        loaded_by(pe, parts_in, N_PARTS, n)
                    openings(t, 1)
                    up_rows(t, "g", 0, 0)
                    up_rows(t, "g", 0, 1)
                    openings(t, 2)
                    up_rows(t, "g", 0, 2)
                    up_rows(t, "g", 0, 3)
                    openings(t, 3)
                    for h in range(HG):
                        for part in range(4):
                            keys_rows(t, h, part)
                            if h < 3:
                                up_rows(t, "ugu"[h], (0, 1, 1)[h], part)
                            else:
                                mlp_down(t, part)
                            if n and part < 3:
                                queries(n, h, part)
                        if h > 0:
                            for part in range(4):
                                values(t, h - 1, part)
                    transposed_weights(t)
                    if n:
                        window(n, 0)
                    experts_down(t, 0)
                    if n:
                        window(n, 1)
                    experts_down(t, 1)
                    for part in range(4):
                        values(t, 3, part)
                steps(pe, step, lead)

        inner = ExitStack()
        with inner:
            sb, ps, sem = make(inner)
            wo = sb("wo", [P, 2, C])
            xr = sb("xr", [P, 2, TT, C])
            yr = sb("yr", [P, 2, TT, C])
            ar = sb("ar", [P, 2, TT, C])
            aT = sb("aT", [P, 2, T])
            res = sb("res", [P, 2, TT, C])
            banks = [ps(f"fbank{i}", [P, 512]) for i in range(8)]
            R = Banks(banks, [sem(f"f_full{i}") for i in range(8)], [sem(f"f_free{i}") for i in range(8)],
                      ["a0", "a1", "o0", "o1"])
            loads = [sem("f_in0"), sem("f_in1")]
            w_in = sem("wo_in")
            sums = Signal(sem("sums"), 1)
            done = Signal(sem("res_stored"), 16, ahead=True)
            armed = sem("armed_f")
            NL = 2 + G

            block = inner.enter_context(nc.Block())

            @block.sync
            def _(sp):
                xv = x.rearrange("b (i p) c -> b p i c", p=P)
                yv = s_y.rearrange("(b i) p c -> b p i c", i=TT)
                av = s_o.rearrange("(b g) i p c -> b g p i c", g=G)

                def load(i, half):
                    for dst, src in ((xr[:, half, :, :], row(xv, i)), (yr[:, half, :, :], row(yv, i))):
                        sp.dma_start(dst, src).then_inc(loads[half], 16)
                    for g in range(G):
                        sp.dma_start(ar[:, half, :, 64 * g:64 * g + 64], row(av, i)[g]).then_inc(loads[half], 16)

                sp.dma_start(wo[:, :, :], Wo.rearrange("(a p) n -> p a n", p=P)).then_inc(w_in, 16)
                load(0, 0)
                sp.wait_ge(armed, 1)

                def turn(t, load_next=True):
                    if load_next:
                        R_before(sp, t)
                        load(t.index + 1, 1 - t.half)

                def R_before(eng, t):
                    R.wait_free(eng, t, "o0")
                    R.wait_free(eng, t, "o1")
                    R.wait_free(eng, t, "a0")
                    R.wait_free(eng, t, "a1")
                with sp.Fori(0, B // 2 - 1) as w:
                    turn(Turn(w, 0))
                    turn(Turn(w, 1))
                turn(Turn(B // 2 - 1, 0))

            @block.gpsimd
            def _(pool):
                for s in R.free[:4]:
                    pool.sem_inc(s, 1)
                pool.sem_inc(done.sem, 16)
                pool.sem_inc(armed, 1)
                with pool.Fori(0, B // 2) as w:
                    for half in range(2):
                        t = Turn(w, half)
                        pool.wait_ge(loads[half], w * (16 * NL) + 16 * NL)
                        nc.gpsimd.tensor_tensor(xr[:, half, :, :], xr[:, half, :, :], yr[:, half, :, :],
                                                ALU.add).then_inc(sums.sem, 1)

            @block.tensor
            def _(pe):
                pe.wait_ge(armed, 1)
                pe.wait_ge(w_in, 16)
                with pe.Fori(0, B // 2) as w:
                    for half in range(2):
                        t = Turn(w, half)
                        pe.wait_ge(loads[half], w * (16 * NL) + 16 * NL)
                        for c in range(2):
                            R.wait_free(pe, t, f"a{c}")
                            for i in range(TT):
                                last = nc.tensor.transpose(R.bank(f"a{c}")[:, i * P:i * P + P],
                                                           ar[:, half, i, c * P:c * P + P], ident[:, :])
                            R.filled(f"a{c}", last)
                        for c in range(2):
                            R.wait_read(pe, t, f"a{c}")
                        for j in range(2):
                            R.wait_free(pe, t, f"o{j}")
                            for i in range(2):
                                for c in range(2):
                                    last = nc.tensor.matmul(R.bank(f"o{j}")[:, i * C:i * C + C],
                                                            aT[:, c, (2 * j + i) * P:(2 * j + i + 1) * P], wo[:, c, :],
                                                            start=(c == 0), stop=(c == 1))
                            R.filled(f"o{j}", last)

            @block.scalar
            def _(act):
                act.wait_ge(armed, 1)
                ov = out.rearrange("b (i p) c -> b p i c", p=P)
                with act.Fori(0, B // 2) as w:
                    for half in range(2):
                        t = Turn(w, half)
                        for c in range(2):
                            R.wait_full(act, t, f"a{c}")
                            if c == 0:
                                R.wait_free(act, t, "o1")
                            R.released(f"a{c}", nc.scalar.activation(aT[:, c, :], R.bank(f"a{c}")[:, :], ACT.Copy))
                        for j in range(2):
                            R.wait_read(act, t, f"o{j}")
                        act.dma_start(row(ov, t.index), res[:, half, :, :]).then_inc(done.sem, 16)
                act.wait_ge(done.sem, 16 * (B + 1))

            @block.vector
            def _(dve):
                dve.wait_ge(armed, 1)
                with dve.Fori(0, B // 2) as w:
                    for half in range(2):
                        t = Turn(w, half)
                        dve.wait_ge(sums.sem, sums.at(t))
                        dve.wait_ge(done.sem, done.before(t))
                        for j in range(2):
                            R.wait_full(dve, t, f"o{j}")
                            R.released(f"o{j}", nc.vector.tensor_tensor(
                                res[:, half, 2 * j:2 * j + 2, :],
                                R.bank(f"o{j}")[:, :].rearrange("p (i c) -> p i c", i=2),
                                xr[:, half, 2 * j:2 * j + 2, :], ALU.add))


_INS = ["L0_attn_x", "L0_attn_Wq", "L0_attn_Wk", "L0_attn_Wv", "L0_attn_Wo", "L0_attn_Wck", "L0_attn_Wcv",
        "L0_attn_Wg", "L0_attn_bg", "L0_ffn_Wg", "L0_ffn_bg", "L0_ffn_Wu", "L0_ffn_bu", "L0_ffn_Wd", "L0_ffn_bd",
        "L0_ffn_Wq", "L0_ffn_keys", "L0_ffn_down_embed", "L0_ffn_up_embed"]


def kernel(**inputs):
    import numpy as _np
    import concourse.bacc as _bacc
    from concourse import mybir as _mybir
    from concourse.bass_utils import run_bass_kernel_spmd as _run

    nc = _bacc.Bacc("TRN2", target_bir_lowering=False, num_devices=1)
    arrays, args = {}, []
    for name in _INS:
        a = _np.ascontiguousarray(inputs[name])
        arrays[f"in_{name}_dram"] = a
        args.append(nc.dram_tensor(f"in_{name}_dram", a.shape, _mybir.dt.from_np(a.dtype), kind="ExternalInput").ap())
    args.append(nc.dram_tensor("out_0_dram", (B, T, C), _mybir.dt.float32, kind="ExternalOutput").ap())
    build(nc, *args)
    r = _run(nc, [arrays], core_ids=[0])
    return r.results[0]["out_0_dram"]
```

```python
import concourse.bass as bass
from concourse import mybir
from contextlib import ExitStack

F32 = mybir.dt.float32
BF16 = mybir.dt.bfloat16
ALU = mybir.AluOpType
ACT = mybir.ActivationFunctionType
AX = mybir.AxisListType

B, T, C = 8, 512, 256
H, D, BLK = 16, 16, 16
NB = T // BLK
WIN = 32
P = 128
TT = T // P
HG = 4
G = H // HG
UNITS = B * G
FF = 1024
FT = FF // P
EX = 1024
XK = EX // 64
PH = 4
KEYS = 64
NEG = -1.0e30
NOT_YET = -1.0e9
LOWEST = -3.0e38
TAKEN = 1.0e30
VW = D + 1


class Signal:

    def __init__(self, sem, per, ahead=False):
        self.sem, self.per, self.ahead = sem, per, ahead

    def at(self, turn, n=None):
        return turn.count(self.per, (self.per if n is None else n) + (self.per if self.ahead else 0))

    def before(self, turn, n=None):
        assert self.ahead
        return turn.count(self.per, self.per if n is None else n)


class Turn:

    def __init__(self, pair, offset, step=0, tail=False):
        self.pair, self.offset, self.half, self.index = pair, offset, offset % 2, pair * 2 + offset
        self.step, self.tail = self if step == 0 else step, tail

    def count(self, per, n):
        return self.pair * (2 * per) + (self.offset * per + n)

    def next(self, ahead=1):
        return Turn(self.pair, self.offset + ahead, step=self)


class Chain:

    def __init__(self, eng, sem, per):
        self.eng, self.sem, self.per, self.n, self.turn = eng, sem, per, 0, None

    def start(self, turn):
        self.turn, self.n = turn, 0

    def link(self, ins):
        self.n += 1
        ins.then_inc(self.sem, 1)
        self.eng.wait_ge(self.sem, self.n if self.turn is None else self.turn.count(self.per, self.n))

    def end(self):
        assert self.n == self.per, f"{self.sem}: {self.n} links in a pass, {self.per} declared"


class Banks:

    def __init__(self, banks, full, free, jobs, front=()):
        self.banks, self.full, self.free, self.jobs, self.front = banks, full, free, jobs, set(front)

    def place(self, job):
        i = self.jobs.index(job)
        return i % len(self.banks), i // len(self.banks)

    def _value(self, turn, job):
        k, before = self.place(job)
        mine = self.jobs[k::len(self.banks)]
        ahead = [j for j in mine if j in self.front]
        if turn.step is None:
            return ahead.index(job) + 1
        if turn.step is turn and job in self.front:
            return turn.count(len(mine), len(ahead) + before + 1 - len(mine))
        if turn.step.tail:
            before = [j for j in mine if j not in self.front].index(job)
        return turn.step.count(len(mine), len(ahead) + before + 1)

    def bank(self, job):
        return self.banks[self.place(job)[0]]

    def wait_free(self, eng, turn, job):
        eng.wait_ge(self.free[self.place(job)[0]], self._value(turn, job))

    def wait_full(self, eng, turn, job):
        eng.wait_ge(self.full[self.place(job)[0]], self._value(turn, job))

    def wait_read(self, eng, turn, job):
        eng.wait_ge(self.free[self.place(job)[0]], self._value(turn, job) + 1)

    def filled(self, job, ins):
        ins.then_inc(self.full[self.place(job)[0]], 1)

    def released(self, job, ins):
        ins.then_inc(self.free[self.place(job)[0]], 1)


def row(ap, index):
    if isinstance(index, int):
        return ap[index]
    names = "abcdef"[:len(ap.shape) - 1]
    return ap[bass.ds(index, 1)].rearrange(f"o {' '.join(names)} -> (o {names[0]}) {' '.join(names[1:])}")


def build(nc, x, Wq, Wk, Wv, Wo, Wck, Wcv, Wg, bg, Fg, fbg, Fu, fbu, Fd, fbd, Rq, keys, down, up, out):
    def dram(name, shape, dt=F32):
        return nc.dram_tensor(name, shape, dt, kind="Internal").ap()

    s_xt = dram("s_xt", [B, P, 2, T])
    s_qf = dram("s_qf", [B, H * D, T])
    s_qs = dram("s_qs", [B, 3, H * D, T], BF16)
    s_ks = dram("s_ks", [B, 3, H * D, T], BF16)
    s_v = dram("s_v", [B, TT, P, H * VW])
    s_kc = dram("s_kc", [B, H * D, HG * NB])
    s_vc = dram("s_vc", [B, G, P, HG * D])
    s_gt = dram("s_gt", [B, P, TT * 3])
    s_o = dram("s_o", [B, TT, P, C])
    s_y = dram("s_y", [UNITS, P, C])

    outer = ExitStack()
    with outer:
        def make(stack):
            def sb(name, shape, dt=F32):
                return stack.enter_context(nc.sbuf_tensor(name, shape, dt))

            def ps(name, shape, dt=F32):
                return stack.enter_context(nc.psum_tensor(name, shape, dt))

            def sem(name):
                return stack.enter_context(nc.semaphore(name))
            return sb, ps, sem

        sb, ps, sem = make(outer)
        ident = sb("ident", [P, P])
        identb = sb("identb", [P, P], BF16)
        causal_ts = sb("causal_ts", [P, P], BF16)
        causal_st = sb("causal_st", [P, 64], BF16)
        window_ts = sb("window_ts", [P, TT, 64], BF16)
        window_st = sb("window_st", [P, P], BF16)
        window_off = sb("window_off", [P, 32], BF16)
        onehot = sb("onehot", [P, T], BF16)
        headones = sb("headones", [P, HG, P], BF16)
        block_ok = sb("block_ok", [P, TT, NB])
        block_no = sb("block_no", [P, TT, NB])
        any_ok = sb("any_ok", [P, TT])
        head_rows = sb("head_rows", [P, HG])
        quad_rows = sb("quad_rows", [P, HG])
        wfg = sb("wfg", [P, 2, FF])
        wfu = sb("wfu", [P, 2, FF])
        wfd = sb("wfd", [P, FT, C])
        wdn = sb("wdn", [P, 2, EX])
        wup = sb("wup", [P, EX // P, C])
        wsim = sb("wsim", [P, 2, 2 * PH * KEYS])
        bias3 = sb("bias3", [96, 2, 2, P], BF16)
        tile_of = sb("tile_of", [96, 4, P], BF16)
        bdb = sb("bdb", [P, C])
        pad = sb("pad", [P, 4])
        units_in = sem("units_in")

        projecting = outer.enter_context(ExitStack())
        sb, _, _ = make(projecting)
        wq = sb("wq", [P, 2, C])
        wk = sb("wk", [P, 2, C])
        wv = sb("wv", [P, 2, C])
        wck = sb("wck", [P, BLK, P])
        wcv = sb("wcv", [P, BLK, P])
        wgate = sb("wgate", [P, 2, 3])
        bgb = sb("bgb", [P, 3])

        inner = ExitStack()
        with inner:
            sb, ps, sem = make(inner)
            wg8 = sb("wg8", [P, 3])
            wqT = sb("wqT", [P, 2, C])
            rq = sb("rq", [P, 2, 512])
            rqT = sb("rqT", [64, 8, C])
            kn = sb("kn", [P, 2, P])
            kT = sb("kT", [64, 2, C])
            dn = sb("dn", [P, EX // P, C])
            b1 = sb("b1", [96, 2, 2, P])
            b2 = sb("b2", [96, 2, 2, P])
            b3 = sb("b3", [96, 2, 2, P], BF16)
            b4 = sb("b4", [96, 2, 2, P], BF16)
            bank = [ps(f"sbank{i}", [P, 512]) for i in range(4)]
            loaded = sem("loaded")
            diag = sem("diag")
            cleared = sem("cleared")
            pool_chain = sem("pool_chain_s")
            dve_chain = sem("dve_chain_s")
            pe_full = sem("pe_full_s")
            read = sem("read_s")
            identity = sem("identity_s")

            block = inner.enter_context(nc.Block())

            @block.sync
            def _(sp):
                for dst, src in (
                        (rq[:, :, :], Rq.rearrange("(a p) n -> p a n", p=P)),
                        (kn[:, :, :], keys.rearrange("(a h) k p n -> (h k) a (p n)", a=2)),
                        (wq[:, :, :], Wq.rearrange("(a p) n -> p a n", p=P)),
                        (dn[:, :, :], down.rearrange("(a p) n -> p a n", p=P)),
                        (wk[:, :, :], Wk.rearrange("(a p) n -> p a n", p=P)),
                        (wv[:, :, :], Wv.rearrange("(a p) n -> p a n", p=P)),
                        (bgb[:, :], bg.rearrange("(o n) -> o n", o=1).broadcast_to([P, 3]))):
                    sp.dma_start(dst, src).then_inc(loaded, 16)
                for h in range(8):
                    sp.dma_start(wg8[16 * h:16 * h + 16, :], Wg).then_inc(loaded, 16)
                sp.wait_ge(cleared, 1)
                for r in range(3):
                    for a, src in enumerate((fbg, fbu)):
                        sp.dma_start(b1[32 * r:32 * r + 4, a, :, :],
                                     src.rearrange("(j k p) -> k j p", j=2, k=4)).then_inc(loaded, 16)
                sp.wait_ge(cleared, 3)
                for dst, src in ((wck, Wck), (wcv, Wcv)):
                    for h in range(8):
                        sp.dma_start(dst[16 * h:16 * h + 16, :, 16 * h:16 * h + 16],
                                     src.rearrange("(j d) e -> d j e", d=D)).then_inc(diag, 16)
                sp.wait_ge(diag, 16 * 16)
                for dst, src in (
                        (wfg[:, :, :], Fg.rearrange("(a p) n -> p a n", p=P)),
                        (wfu[:, :, :], Fu.rearrange("(a p) n -> p a n", p=P)),
                        (wfd[:, :, :], Fd.rearrange("(a p) n -> p a n", p=P)),
                        (wup[:, :, :], up.rearrange("(a p) n -> p a n", p=P)),
                        (bdb[:, :], fbd.rearrange("(o n) -> o n", o=1).broadcast_to([P, C]))):
                    sp.dma_start(dst, src).then_inc(units_in, 16)

            @block.gpsimd
            def _(pool):
                ch = Chain(pool, pool_chain, 0)
                g = nc.gpsimd

                def keep(ap, pattern, base, cm, fill, op=ALU.is_ge):
                    ch.link(g.affine_select(out=ap, in_=ap, compare_op=op, fill=fill, base=base,
                                            pattern=pattern, channel_multiplier=cm))
                g.memset(b1[:, :, :, :], 0.0).then_inc(cleared, 1)
                g.memset(wck[:, :, :], 0.0).then_inc(cleared, 1)
                g.memset(wcv[:, :, :], 0.0).then_inc(cleared, 1)
                for m in (ident, identb):
                    ch.link(g.memset(m[:, :], 0.0))
                    g.affine_select(out=m[:, :], in_=m[:, :], compare_op=ALU.not_equal, fill=1.0, base=0,
                                    pattern=[[-1, P]], channel_multiplier=1).then_inc(identity, 1)
                for m in (causal_ts, causal_st, window_st, window_off):
                    g.memset(m[:, :], 0.0)
                ch.link(g.memset(window_ts[:, :, :], 0.0))
                keep(causal_ts[:, 0:64], [[-1, 64]], 0, 1, NEG)
                keep(causal_st[:, :], [[1, 64]], 0, -1, NEG)
                keep(window_st[:, :], [[1, P]], 0, -1, NEG)
                keep(window_st[:, :], [[-1, P]], WIN, 1, NEG)
                keep(window_off[96:128, :], [[-1, 32]], 0, 1, NEG)
                g.memset(onehot[:, :], 1.0)
                ch.link(g.memset(headones[:, :, :], 0.0))
                for q in range(4):
                    rows = slice(32 * q, 32 * q + 32)
                    ch.link(g.memset(headones[rows, q, :], 1.0))
                ch.link(g.memset(tile_of[:, :, :], 1.0))
                for r in range(3):
                    rows = slice(32 * r, 32 * r + 32)
                    keep(tile_of[rows, :, :], [[-1, 4], [0, P]], 0, 1, 0.0)
                    keep(tile_of[rows, :, :], [[1, 4], [0, P]], 0, -1, 0.0)
                for m in (block_ok, any_ok, head_rows, quad_rows):
                    g.memset(m[:], 1.0)
                ch.link(g.memset(block_no[:, :, :], 0.0))
                for q in range(4):
                    rows = slice(32 * q, 32 * q + 32)
                    keep(window_ts[rows, :, :], [[0, TT], [1, 64]], 0, -1, NEG)
                    keep(window_ts[rows, :, :], [[0, TT], [-1, 64]], WIN, 1, NEG)
                keep(onehot[96:128, :], [[1, T]], 0, -BLK, 0.0)
                keep(onehot[96:128, :], [[-1, T]], BLK - 1, BLK, 0.0)
                keep(onehot[96:128, :], [[0, T]], NB - 2, -1, 1.0)
                ch.link(g.memset(window_ts[0:32, 0, 0:32], NEG))
                keep(block_ok[:, :, :], [[P, TT], [-BLK, NB]], -BLK, 1, 0.0)
                keep(block_no[:, :, :], [[P, TT], [-BLK, NB]], -BLK, 1, NOT_YET)
                keep(any_ok[:, :], [[P, TT]], -BLK, 1, 0.0)
                for rows in (slice(0, 64), slice(64, 128)):
                    keep(head_rows[rows, :], [[-D, HG]], 0, 1, 0.0)
                    keep(head_rows[rows, :], [[D, HG]], D - 1, -1, 0.0)
                keep(quad_rows[:, :], [[-32, HG]], 0, 1, 0.0)
                keep(quad_rows[:, :], [[32, HG]], 31, -1, 0.0)

            jobs = ([("wqT", h) for h in range(2)] + [("rqT", i) for i in range(4)] + [("kT", 0)]
                    + [("dn", c, n) for c in range(2) for n in range(2)] + [("wgate",)]
                    + [("wsim", c) for c in range(2)])

            @block.tensor
            def _(pe):
                pe.wait_ge(loaded, 21 * 16)
                pe.wait_ge(identity, 2)
                for i, job in enumerate(jobs):
                    b = bank[i % 4]
                    if i >= 4:
                        pe.wait_ge(read, i - 3)
                    if job[0] == "wgate":
                        pe.wait_ge(read, 2)
                    if job[0] == "wsim":
                        pe.wait_ge(read, 7)
                    if job[0] == "wqT":
                        for c in range(2):
                            last = nc.tensor.transpose(b[:, c * P:c * P + P], wq[:, c, job[1] * P:job[1] * P + P], ident[:, :])
                    elif job[0] == "rqT":
                        for k in range(2):
                            for c in range(2):
                                o = 64 * (2 * job[1] + k)
                                last = nc.tensor.transpose(b[0:64, (2 * k + c) * P:(2 * k + c + 1) * P],
                                                           rq[:, c, o:o + 64], ident[:, :])
                    elif job[0] == "kT":
                        for p in range(2):
                            for a in range(2):
                                last = nc.tensor.transpose(b[0:64, (2 * p + a) * P:(2 * p + a + 1) * P],
                                                           kn[:, a, 64 * p:64 * p + 64], ident[:, :])
                    elif job[0] == "dn":
                        _n, c, n = job
                        for e in range(4):
                            last = nc.tensor.transpose(b[:, e * P:e * P + P],
                                                       dn[:, 4 * n + e, c * P:c * P + P], ident[:, :])
                    elif job[0] == "wgate":
                        for c in range(2):
                            for h in range(2):
                                last = nc.tensor.matmul(b[:, 4 * c:4 * c + 3], wqT[:, h, c * P:c * P + P],
                                                        wg8[:, :], start=(h == 0), stop=(h == 1))
                    else:
                        for i8 in range(8):
                            p, h = divmod(i8, PH)
                            last = nc.tensor.matmul(b[:, 64 * i8:64 * i8 + 64],
                                                    rqT[:, i8, job[1] * P:job[1] * P + P],
                                                    kT[:, p, 64 * h:64 * h + 64], start=True, stop=True)
                    last.then_inc(pe_full, 1)

            @block.vector
            def _(dve):
                ch = Chain(dve, dve_chain, 0)
                v = nc.vector
                dve.wait_ge(loaded, 21 * 16)
                ch.link(v.tensor_copy(b3[:, :, :, :], b1[:, :, :, :]))
                v.tensor_copy(bias3[0:32, :, :, :], b3[0:32, :, :, :])
                ch.link(v.tensor_tensor(b2[:, :, :, :], b1[:, :, :, :], b3[:, :, :, :], ALU.subtract))
                ch.link(v.tensor_copy(b4[:, :, :, :], b2[:, :, :, :]))
                v.tensor_copy(bias3[32:64, :, :, :], b4[32:64, :, :, :])
                v.tensor_tensor(bias3[64:96, :, :, :], b2[64:96, :, :, :], b4[64:96, :, :, :], ALU.subtract)
                for i, job in enumerate(jobs):
                    b = bank[i % 4]
                    dve.wait_ge(pe_full, i + 1)
                    if job[0] == "wqT":
                        last = v.tensor_copy(wqT[:, job[1], :], b[:, 0:C])
                    elif job[0] == "rqT":
                        last = v.tensor_copy(rqT[:, 2 * job[1]:2 * job[1] + 2, :],
                                             b[0:64, :].rearrange("p (k n) -> p k n", k=2))
                    elif job[0] == "kT":
                        last = v.tensor_copy(kT[:, :, :], b[0:64, :].rearrange("p (k n) -> p k n", k=2))
                    elif job[0] == "dn":
                        last = v.tensor_copy(wdn[:, job[1], job[2] * 512:job[2] * 512 + 512], b[:, :])
                    elif job[0] == "wgate":
                        last = v.tensor_scalar(wgate[:, :, :], b[:, 0:8].rearrange("p (a n) -> p a n", a=2)[:, :, 0:3],
                                               1.0 / H, None, ALU.mult)
                    else:
                        last = v.tensor_copy(wsim[:, job[1], :], b[:, :])
                    last.then_inc(read, 1)

        inner = ExitStack()
        with inner:
            sb, ps, sem = make(inner)
            xin = sb("xin", [P, 2, TT, C])
            stats = sb("stats", [P, TT, 6])
            mv = sb("mv", [P, TT, 2])
            std = sb("std", [P, TT])
            eps = sb("eps", [P, 1])
            rstd = sb("rstd", [P, TT])
            xn = sb("xn", [P, TT, C])
            xT = sb("xT", [P, 2, 2, T])
            qk = sb("qk", [P, 2, 2, 2, T])
            rem = sb("rem", [P, 2, 2, T])
            parts = sb("parts", [P, 2, 3, 2, T], BF16)
            vn = sb("vn", [P, TT, C])
            vo = sb("vo", [P, TT, H, VW])
            vT = sb("vT", [P, 2, T])
            kcs = sb("kcs", [P, 2, HG, NB])
            vcr = sb("vcr", [P, 2, HG, NB])
            vcs = sb("vcs", [P, 2, 2, HG, D])
            gl = sb("gl", [P, TT, 3])
            gm = sb("gm", [P, TT])
            gs = sb("gs", [P, TT])
            NBK = 8
            banks = [ps(f"tbank{i}", [P, 512]) for i in range(NBK)]
            R = Banks(banks, [sem(f"t_full{i}") for i in range(NBK)], [sem(f"t_free{i}") for i in range(NBK)],
                      ["x0", "x1", "w0", "w1", "q0", "q1", "k0", "k1", "kv", "v0", "v1", "gt", "vc"],
                      front=["x0", "x1", "q0", "q1", "k0", "k1", "v0", "v1"])
            x_in = [sem("x_in0"), sem("x_in1")]
            std_ready = Signal(sem("std_ready"), 1)
            var_ready = Signal(sem("var_ready"), 1)
            xn_ready = Signal(sem("xn_ready"), TT)
            part_hi = Signal(sem("part_hi"), 2)
            part_mid = Signal(sem("part_mid"), 2)
            part_lo = Signal(sem("part_lo"), 2, ahead=True)
            rem_hi = Signal(sem("rem_hi"), 2)
            rem_mid = Signal(sem("rem_mid"), 2)
            kc_ready = Signal(sem("kc_ready"), 2)
            gate_in = Signal(sem("gate_in"), 1)
            gate_exp = Signal(sem("gate_exp"), 1)
            gate_ready = Signal(sem("gate_ready"), 1)
            stored = {n: Signal(sem(f"st_{n}"), 16 * k, ahead=True) for n, k in
                      (("xt", 1), ("qf", 1), ("parts", 2), ("v", 1), ("kc", 1), ("vc", 1), ("gt", 1))}
            dve_chain = sem("dve_chain_t")
            ln_chain = sem("ln_chain")
            armed = sem("armed_t")
            constants = sem("constants_t")
            carried = sem("carried_t")

            def steps(eng, step, lead=None):
                if lead:
                    lead(Turn(0, 0, step=None))
                with eng.Fori(0, B // 2 - 1) as w:
                    for half in range(2):
                        t = Turn(w, half)
                        step(t, t.next(), t.next(2))
                t = Turn(B // 2 - 1, 0)
                step(t, t.next(), None)
                step(Turn(B // 2 - 1, 1, tail=True), None, None)

            block = inner.enter_context(nc.Block())

            @block.sync
            def _(sp):
                xv = x.rearrange("b (i p) c -> b p i c", p=P)
                for half in range(2):
                    sp.dma_start(xin[:, half, :, :], xv[half]).then_inc(x_in[half], 16)
                sp.wait_ge(armed, 1)

                def store(name, dst, src):
                    sp.sem_inc(carried, 1)
                    sp.dma_start(dst, src).then_inc(stored[name].sem, 16)

                def store_tokens(n):
                    R.wait_read(sp, n, "x1")
                    store("xt", row(s_xt, n.index), xT[:, n.half, :, :])

                def store_products(n):
                    R.wait_read(sp, n, "q1")
                    store("qf", row(s_qf, n.index).rearrange("(h r) t -> r h t", h=2), qk[:, n.half, 0, :, :])
                    R.wait_read(sp, n, "v1")
                    store("v", row(s_v, n.index).rearrange("i p n -> p i n"),
                          vo[:, :, :, :].rearrange("p i h d -> p i (h d)"))

                def store_parts(n):
                    for a, dst in ((0, s_qs), (1, s_ks)):
                        sp.wait_ge(part_lo.sem, part_lo.at(n, a + 1))
                        store("parts", row(dst, n.index).rearrange("r (h p) t -> p r h t", h=2), parts[:, a, :, :, :])

                def lead(n):
                    store_tokens(n)
                    store_products(n)
                    store_parts(n)

                def step(t, n, after):
                    i = t.index
                    if after:
                        sp.wait_ge(xn_ready.sem, xn_ready.at(t))
                        sp.dma_start(xin[:, t.half, :, :], row(xv, i + 2)).then_inc(x_in[t.half], 16)
                    if n:
                        store_tokens(n)
                    sp.wait_ge(kc_ready.sem, kc_ready.at(t))
                    store("kc", row(s_kc, i).rearrange("(h r) n -> r h n", h=2), kcs[:, :, :, :].rearrange("p h a n -> p h (a n)"))
                    if n:
                        store_products(n)
                    R.wait_read(sp, t, "vc")
                    store("vc", row(s_vc, i).rearrange("g p n -> p g n"),
                          vcs[:, :, :, :, :].rearrange("p h g a d -> p (h g) (a d)"))
                    sp.wait_ge(gate_ready.sem, gate_ready.at(t))
                    store("gt", row(s_gt, i), gl[:, :, :].rearrange("p i n -> p (i n)"))
                    if n:
                        store_parts(n)
                steps(sp, step, lead)
                for s in stored.values():
                    sp.wait_ge(s.sem, s.per * (B + 1))

            @block.gpsimd
            def _(pool):
                g = nc.gpsimd
                for s in (part_lo, *stored.values()):
                    pool.sem_inc(s.sem, s.per)
                for s in R.free:
                    pool.sem_inc(s, 1)
                g.memset(eps[:, :], 1e-5).then_inc(constants, 1)
                g.memset(vo[:, :, :, D:VW], 1.0).then_inc(constants, 1)
                pool.sem_inc(armed, 1)
                with pool.Fori(0, B // 2) as w:
                    for half in range(2):
                        t = Turn(w, half)
                        for a in range(2):
                            pool.wait_ge(part_lo.sem, part_lo.before(t, a + 1))
                            pool.wait_ge(part_hi.sem, part_hi.at(t, a + 1))
                            g.tensor_tensor(rem[:, a, :, :], qk[:, half, a, :, :], parts[:, a, 0, :, :],
                                            ALU.subtract).then_inc(rem_hi.sem, 1)
                        for a in range(2):
                            pool.wait_ge(rem_hi.sem, rem_hi.at(t, a + 1))
                            pool.wait_ge(part_mid.sem, part_mid.at(t, a + 1))
                            g.tensor_tensor(rem[:, a, :, :], rem[:, a, :, :], parts[:, a, 1, :, :],
                                            ALU.subtract).then_inc(rem_mid.sem, 1)

            @block.scalar
            def _(act):
                s = nc.scalar
                act.wait_ge(armed, 1)
                act.wait_ge(constants, 2)
                def deviation(t):
                    act.wait_ge(var_ready.sem, var_ready.at(t))
                    s.activation(std[:, :], mv[:, :, 1], ACT.Sqrt, bias=eps[:, 0:1]).then_inc(std_ready.sem, 1)

                def split(n):
                    act.wait_ge(stored["qf"].sem, stored["qf"].before(n))
                    act.wait_ge(stored["parts"].sem, stored["parts"].before(n))
                    for a, name in ((0, "q"), (1, "k")):
                        for h in range(2):
                            job = f"{name}{h}"
                            R.wait_full(act, n, job)
                            R.released(job, s.activation(qk[:, n.half, a, h, :], R.bank(job)[:, :],
                                                         ACT.Copy, scale=0.25 if a == 0 else 1.0))
                        for h in range(2):
                            R.wait_read(act, n, f"{name}{h}")
                        s.activation(parts[:, a, 0, :, :], qk[:, n.half, a, :, :], ACT.Copy).then_inc(part_hi.sem, 1)
                    for a in range(2):
                        act.wait_ge(rem_hi.sem, rem_hi.at(n, a + 1))
                        s.activation(parts[:, a, 1, :, :], rem[:, a, :, :], ACT.Copy).then_inc(part_mid.sem, 1)

                def low_parts(n):
                    for a in range(2):
                        act.wait_ge(rem_mid.sem, rem_mid.at(n, a + 1))
                        s.activation(parts[:, a, 2, :, :], rem[:, a, :, :], ACT.Copy).then_inc(part_lo.sem, 1)

                def lead(n):
                    deviation(n)
                    deviation(Turn(0, 1))
                    split(n)
                    low_parts(n)

                def step(t, n, after):
                    for h in range(2):
                        R.wait_full(act, t, f"w{h}")
                        R.released(f"w{h}", s.activation(vT[:, h, :], R.bank(f"w{h}")[:, :], ACT.Copy))
                    if n:
                        split(n)
                    if after:
                        deviation(after)
                    act.wait_ge(gate_in.sem, gate_in.at(t))
                    s.activation(gl[:, :, :], gl[:, :, :], ACT.Exp).then_inc(gate_exp.sem, 1)
                    if n:
                        low_parts(n)
                steps(act, step, lead)

            @block.vector
            def _(dve):
                v = nc.vector
                dve.wait_ge(armed, 1)
                dve.wait_ge(constants, 2)
                ch = Chain(dve, dve_chain, 4)
                cl = Chain(dve, ln_chain, 2)

                def statistics(t):
                    cl.start(t)
                    dve.wait_ge(x_in[t.half], t.pair * 16 + (t.offset // 2 * 16 + 16))
                    for i in range(TT):
                        last = v.bn_stats(stats[:, i, :], xin[:, t.half, i, :])
                    cl.link(last)
                    v.memset(pad[:, 0:1], 0.0)
                    for i in range(TT):
                        last = v.bn_aggr(mv[:, i, :], stats[:, i, :])
                    last.then_inc(var_ready.sem, 1)

                def normalize(t):
                    dve.wait_ge(std_ready.sem, std_ready.at(t))
                    cl.link(v.reciprocal(rstd[:, :], std[:, :]))
                    for i in range(TT):
                        v.tensor_scalar(xn[:, i, :], xin[:, t.half, i, :], mv[:, i, 0:1], rstd[:, i:i + 1],
                                        ALU.subtract, ALU.mult).then_inc(xn_ready.sem, 1)
                    cl.end()

                def tokens(n):
                    dve.wait_ge(stored["xt"].sem, stored["xt"].before(n))
                    for c in range(2):
                        R.wait_full(dve, n, f"x{c}")
                        R.released(f"x{c}", v.tensor_copy(xT[:, n.half, c, :], R.bank(f"x{c}")[:, :]))

                def values(n):
                    dve.wait_ge(stored["v"].sem, stored["v"].before(n))
                    for j in range(2):
                        R.wait_full(dve, n, f"v{j}")
                        for i in range(2):
                            v.tensor_copy(vo[:, 2 * j + i, :, 0:D],
                                          R.bank(f"v{j}")[:, i * C:i * C + C].rearrange("p (h d) -> p h d", h=H))
                        last = v.tensor_copy(vn[:, 2 * j:2 * j + 2, :], R.bank(f"v{j}")[:, :].rearrange("p (i n) -> p i n", i=2))
                        R.released(f"v{j}", last)

                def compressed(t):
                    R.wait_full(dve, t, "kv")
                    dve.wait_ge(stored["kc"].sem, stored["kc"].before(t))
                    kv = R.bank("kv")
                    for h in range(2):
                        v.tensor_tensor(kcs[:, h, :, :], kv[:, None, NB * h:NB * h + NB].broadcast_to([P, HG, NB]),
                                        head_rows[:, :, None].broadcast_to([P, HG, NB]), ALU.mult)\
                         .then_inc(kc_ready.sem, 1)
                        last = v.tensor_copy(vcr[:, h, :, :], kv[:, None, NB * (2 + h):NB * (3 + h)]
                                             .broadcast_to([P, HG, NB]))
                    R.released("kv", last)

                def gates_in(t):
                    ch.start(t)
                    R.wait_full(dve, t, "gt")
                    dve.wait_ge(stored["gt"].sem, stored["gt"].before(t))
                    R.released("gt", v.tensor_tensor(
                        gl[:, :, :], R.bank("gt")[:, 0:16].rearrange("p (i n) -> p i n", i=TT)[:, :, 0:3],
                        bgb[:, None, :].broadcast_to([P, TT, 3]), ALU.add))
                    R.wait_read(dve, t, "gt")
                    ch.link(v.tensor_reduce(gm[:, :], gl[:, :, :], AX.X, ALU.max))
                    v.tensor_tensor(gl[:, :, :], gl[:, :, :], gm[:, :, None].broadcast_to([P, TT, 3]),
                                    ALU.subtract).then_inc(gate_in.sem, 1)

                def compressed_values(t):
                    dve.wait_ge(stored["vc"].sem, stored["vc"].before(t))
                    R.wait_full(dve, t, "vc")
                    for h in range(2):
                        last = v.tensor_tensor(
                            vcs[:, h, :, :, :], R.bank("vc")[:, P * h:P * h + P].rearrange("p (g h d) -> p g h d", g=2, h=HG),
                            quad_rows[:, None, :, None].broadcast_to([P, 2, HG, D]), ALU.mult)
                    R.released("vc", last)

                def gates_out(t):
                    dve.wait_ge(gate_exp.sem, gate_exp.at(t))
                    ch.link(v.tensor_reduce(gs[:, :], gl[:, :, :], AX.X, ALU.add))
                    ch.link(v.reciprocal(gm[:, :], gs[:, :]))
                    ch.link(v.tensor_tensor(gl[:, :, :], gl[:, :, :], gm[:, :, None].broadcast_to([P, TT, 3]), ALU.mult))
                    v.tensor_tensor(gl[:, :, 0], gl[:, :, 0], any_ok[:, :], ALU.mult).then_inc(gate_ready.sem, 1)
                    ch.end()

                def lead(n):
                    statistics(n)
                    normalize(n)
                    tokens(n)
                    statistics(Turn(0, 1))
                    normalize(Turn(0, 1))
                    values(n)

                def step(t, n, after):
                    if n:
                        tokens(n)
                    if after:
                        statistics(after)
                    compressed(t)
                    if n:
                        values(n)
                    if after:
                        normalize(after)
                    gates_in(t)
                    compressed_values(t)
                    gates_out(t)
                steps(dve, step, lead)

            @block.tensor
            def _(pe):
                mm, tr = nc.tensor.matmul, nc.tensor.transpose
                pe.wait_ge(armed, 1)

                def transposed_tokens(n):
                    for c in range(2):
                        R.wait_free(pe, n, f"x{c}")
                        for i in range(TT):
                            if c == 0:
                                pe.wait_ge(xn_ready.sem, xn_ready.at(n, i + 1))
                            last = tr(R.bank(f"x{c}")[:, i * P:i * P + P], xn[:, i, c * P:c * P + P], ident[:, :])
                        R.filled(f"x{c}", last)

                def transposed_values(t):
                    for j in range(2):
                        R.wait_read(pe, t, f"v{j}")
                    for h in range(2):
                        R.wait_free(pe, t, f"w{h}")
                        for i in range(TT):
                            last = tr(R.bank(f"w{h}")[:, i * P:i * P + P], vn[:, i, P * h:P * h + P], ident[:, :])
                        R.filled(f"w{h}", last)

                def queries_keys(n):
                    for c in range(2):
                        R.wait_read(pe, n, f"x{c}")
                    for name, wt in (("q", wq), ("k", wk)):
                        for h in range(2):
                            job = f"{name}{h}"
                            R.wait_free(pe, n, job)
                            for c in range(2):
                                last = mm(R.bank(job)[:, :], wt[:, c, h * P:h * P + P], xT[:, n.half, c, :],
                                          start=(c == 0), stop=(c == 1))
                            R.filled(job, last)

                def compress(t):
                    R.wait_free(pe, t, "kv")
                    for kind in range(2):
                        for h in range(2):
                            R.wait_read(pe, t, f"{'kw'[kind]}{h}")
                        src = (qk[:, t.half, 1, :, :] if kind == 0 else vT[:, :, :]).rearrange("p h (n j) -> p h n j", j=BLK)
                        for j in range(BLK):
                            last = mm(R.bank("kv")[:, 2 * NB * kind:2 * NB * (kind + 1)], (wck, wcv)[kind][:, j, :],
                                      src[:, :, :, j], start=(j == 0), stop=(j == BLK - 1))
                    R.filled("kv", last)

                def values(n):
                    for j in range(2):
                        R.wait_free(pe, n, f"v{j}")
                        for i in range(2):
                            for c in range(2):
                                last = mm(R.bank(f"v{j}")[:, i * C:i * C + C],
                                          xT[:, n.half, c, (2 * j + i) * P:(2 * j + i + 1) * P],
                                          wv[:, c, :], start=(c == 0), stop=(c == 1))
                        R.filled(f"v{j}", last)

                def gates(t):
                    R.wait_free(pe, t, "gt")
                    for i in range(TT):
                        for c in range(2):
                            last = mm(R.bank("gt")[:, 4 * i:4 * i + 3], xT[:, t.half, c, i * P:i * P + P], wgate[:, c, :],
                                      start=(c == 0), stop=(c == 1))
                    R.filled("gt", last)

                def compressed_values(t):
                    R.wait_free(pe, t, "vc")
                    R.wait_read(pe, t, "kv")
                    for h in range(2):
                        last = mm(R.bank("vc")[:, P * h:P * h + P], vcr[:, h, :, :].rearrange("p r n -> p (r n)"),
                                  ident[:, :], start=True, stop=True)
                    R.filled("vc", last)

                def lead(n):
                    transposed_tokens(n)
                    queries_keys(n)
                    values(n)

                def step(t, n, after):
                    if n:
                        transposed_tokens(n)
                    transposed_values(t)
                    if n:
                        queries_keys(n)
                    compress(t)
                    if n:
                        values(n)
                    gates(t)
                    compressed_values(t)
                steps(pe, step, lead)
        projecting.close()

        inner = ExitStack()
        with inner:
            sb, ps, sem = make(inner)
            SP3 = 96
            qo = sb("qo", [P, 2, HG, T], BF16)
            ko = sb("ko", [P, 2, HG, T], BF16)
            qf = sb("qf", [64, 2, T])
            kc = sb("kc", [64, 2, P])
            vc = sb("vc", [P, 2, HG * D])
            vv = sb("vv", [P, 2, TT, HG, VW])
            gt = sb("gt", [P, 2, TT, 3])
            xb = sb("xb", [P, 2, C])
            xt = sb("xt", [P, 2, 2, P])
            lc = sb("lc", [P, TT, HG, NB + 4])
            top = sb("top", [P, TT, HG, 8])
            strike = sb("strike", [P, TT, HG, 8])
            struck = sb("struck", [P, TT, HG, NB + 4])
            pc = sb("pc", [P, TT, HG, NB])
            csum = sb("csum", [P, TT * HG])
            cfac = sb("cfac", [P, TT, HG])
            pcT = sb("pcT", [P, T])
            co = sb("co", [P, TT, HG * D])
            unsel = sb("unsel", [P, TT, HG, NB], BF16)
            bmax = sb("bmax", [P, TT, HG, NB])
            bsel = sb("bsel", [P, TT, HG, NB])
            smax = sb("smax", [P, TT * HG])
            smax_hi = sb("smax_hi", [P, TT * HG], BF16)
            lmax = sb("lmax", [P, HG * TT])
            shift_s = sb("shift_s", [P, TT, HG, NB], BF16)
            shift_l = sb("shift_l", [P, TT, HG, NB], BF16)
            shiftT = sb("shiftT", [P, T], BF16)
            OFFS = [0, 512, 896, 1152]
            pts = sb("pts", [P, 2, 1280])
            ptl = sb("ptl", [P, 2, T])
            pto = sb("pto", [P, HG, TT - 1, 32])
            rs = sb("rs", [P, 4 * TT])
            fs = sb("fs", [P, 4 * TT])
            on = sb("on", [P, 2, 4 * TT, D])
            at = sb("at", [P, TT, HG, D])
            th = sb("th", [P, 2, 512])
            gs = sb("gated", [P, 2, 512])
            hT = sb("hT", [P, FT, P])
            sim = sb("sim", [P, 2, PH, KEYS])
            t8 = sb("t8", [P, 2, PH, 8])
            marks = sb("marks", [P, 2, PH, KEYS])
            xy = sb("xy", [P, 2, PH, KEYS])
            cand = sb("cand", [P, PH, 8, 8])
            c8 = sb("c8", [P, PH, 8])
            e8 = sb("e8", [P, PH, 8])
            esum = sb("esum", [P, PH])
            erec = sb("erec", [P, PH])
            nmax = sb("nmax", [P, PH])
            sumxy = sb("sumxy", [P, PH, XK, KEYS])
            ex = sb("ex", [P, 2, EX])
            mw = sb("mw", [P, 2, EX])
            cw = sb("cw", [P, EX])
            csm = sb("csm", [P, 1])
            clast = sb("clast", [P, 1])
            tw = sb("tw", [P, 2, 512])
            sw = sb("sw", [P, EX])
            cwT = sb("cwT", [P, EX // P, P])
            yo = sb("yo", [P, C])

            q_jobs = ["lc"] + [f"p{h}{k}" for h in range(HG) for k in (3, 0, 1)] + ["m0", "m1"]
            k_jobs = ["aug", "pcT", "off", "a0", "co"]
            for h in range(HG):
                k_jobs += [f"s{h}0", f"s{h}1", f"s{h}2"] + [f"a{h + 1}"] * (h < HG - 1) + [f"d{h}"]

            def ring(name, n, jobs, front=()):
                return Banks([ps(f"{name}_bank{i}", [P, 512]) for i in range(n)],
                             [sem(f"{name}_full{i}") for i in range(n)],
                             [sem(f"{name}_read{i}") for i in range(n)], jobs, front)
            Q = ring("q", 2, q_jobs, front=q_jobs)
            K = ring("k", 2, k_jobs)
            F = ring("f", 2, ["w0", "w1", "sim", "g0", "u0", "g1", "u1", "t0", "t1"], front=["sim"])
            O = ring("o", 1, ["o0", "o1"])
            Y = ring("y", 1, ["y"])
            near_in = [sem("near_in0"), sem("near_in1")]
            parts_in = [sem("parts_in0"), sem("parts_in1")]
            late_in = [sem("late_in0"), sem("late_in1")]
            N_NEAR, N_PARTS, N_LATE = 3, 12, 4
            S = {}
            for name, per, ahead in (
                    ("lc_done", 1, 0), ("top_done", 1, 0), ("strike_done", 1, 0),
                    ("pc_in", 1, 0), ("pc_exp", 1, 0), ("cfac_done", 1, 0), ("pc_done", 1, 0),
                    ("smax_done", 1, 0), ("shift_lo", 1, 0), ("shift_done", 1, 0),
                    ("xb_done", 1, 0), ("pv", HG, 1), ("at_sum", 2, 0), ("at_done", 1, 1),
                    ("th_done", 2, 0), ("t8_done", 1, 0), ("xy_in", 1, 0), ("xy_done", 1, 0), ("cand_done", 1, 0),
                    ("c8_done", 1, 0), ("e8_in", 1, 0), ("e8_exp", 1, 0), ("nmax_done", 1, 0), ("sum_done", PH, 0),
                    ("ex_done", PH, 0), ("mw_done", PH, 0), ("cw_sum", PH - 1, 0), ("clast_done", 1, 0),
                    ("cw_done", 1, 0), ("tw_done", 2, 0), ("st_at", 16, 1), ("st_y", 16, 1)):
                S[name] = Signal(sem(name), per, ahead=bool(ahead))
            armed = sem("armed_u")
            carried = sem("carried")
            key_blocks = sem("key_blocks")
            near_chain, far_chain = sem("near_chain"), sem("far_chain")
            constants = sem("constants_u")

            def need(eng, name, t, n=None):
                eng.wait_ge(S[name].sem, S[name].at(t, n))

            def need_before(eng, name, t, n=None):
                eng.wait_ge(S[name].sem, S[name].before(t, n))

            def done(name, ins):
                ins.then_inc(S[name].sem, 1)

            def steps(eng, step, lead=None):
                if lead:
                    lead(Turn(0, 0, step=None))
                with eng.Fori(0, UNITS // 2 - 1) as w:
                    step(Turn(w, 0))
                    step(Turn(w, 1))
                step(Turn(UNITS // 2 - 1, 0))
                step(Turn(UNITS // 2 - 1, 1, tail=True))

            def loaded_by(eng, lot, n, t):
                eng.wait_ge(lot[t.half], t.pair * (16 * n) + 16 * n * (t.offset // 2 + 1))

            block = inner.enter_context(nc.Block())

            @block.sync
            def _(sp):
                qs, ks = (a.rearrange("b r (g h d) t -> b g r d h t", g=G, d=D) for a in (s_qs, s_ks))
                qff = s_qf.rearrange("b (g p) t -> b g p t", g=G)
                kcf = s_kc.rearrange("b (g p) n -> b g p n", g=G)
                vf = s_v.rearrange("b i p (g n) -> b g p i n", g=G)

                tiles = x.rearrange("b (i p) c -> b i p c", p=P)

                def send(pairs, to, n):
                    assert len(pairs) == n
                    for dst, src in pairs:
                        sp.dma_start(dst, src).then_inc(to, 16)

                def load_near(b, g, half):
                    send([(qf[:, half, :], row(qff, b)[g]), (kc[:, half, :], row(kcf, b)[g]),
                          (xt[:, half, :, :], row(s_xt, b)[:, :, g * P:g * P + P])], near_in[half], N_NEAR)

                def load_parts(b, g, half):
                    q, k = row(qs, b)[g], row(ks, b)[g]
                    send([(to[D * n:D * n + D, half, :, :], src[r]) for to, src, parts in ((qo, q, (0, 0, 0, 1, 1, 2)), (ko, k, (0, 1, 2, 0, 1, 0)))
                          for n, r in enumerate(parts)], parts_in[half], N_PARTS)

                def load_late(b, g, half):
                    send([(vc[:, half, :], row(s_vc, b)[g]),
                          (vv[:, half, :, :, :].rearrange("p i h d -> p i (h d)"), row(vf, b)[g]),
                          (gt[:, half, :, :].rearrange("p i n -> p (i n)"), row(s_gt, b)),
                          (xb[:, half, :], row(tiles, b)[g])], late_in[half], N_LATE)

                for u in range(2):
                    load_near(0, u, u)
                    load_parts(0, u, u)
                    load_late(0, u, u)
                sp.wait_ge(armed, 1)

                def step(t, b_now, g_now, load_next=True):
                    half = t.half
                    b, g = (b_now, g_now + 2) if g_now < 2 else (b_now + 1, g_now - 2)
                    if load_next:
                        F.wait_full(sp, t, "u1")
                        load_near(b, g, half)
                        K.wait_full(sp, t, "d3")
                        load_parts(b, g, half)
                        O.wait_read(sp, t, "o1")
                        load_late(b, g, half)
                    need(sp, "at_done", t)
                    sp.sem_inc(carried, 1)
                    sp.dma_start(row(s_o, b_now)[:, :, HG * D * g_now:HG * D * (g_now + 1)].rearrange("i p n -> p i n"),
                                 at[:, :, :, :].rearrange("p i h d -> p i (h d)")).then_inc(S["st_at"].sem, 16)
                    Y.wait_read(sp, t, "y")
                    sp.dma_start(row(s_y.rearrange("(b g) p c -> b g p c", g=G), b_now)[g_now], yo[:, :]).then_inc(S["st_y"].sem, 16)

                def four(b, last=False):
                    for g in range(G):
                        t = Turn(b * 2 + g // 2, g % 2, tail=last and g == G - 1)
                        step(t, b, g, load_next=not last or g < 2)

                with sp.Fori(0, B - 1) as b:
                    four(b)
                four(B - 1, last=True)
                for n in ("st_at", "st_y"):
                    sp.wait_ge(S[n].sem, 16 * (UNITS + 1))

            @block.gpsimd
            def _(pool):
                g_ = nc.gpsimd
                for s in S.values():
                    if s.ahead:
                        pool.sem_inc(s.sem, s.per)
                for r in (Q, K, F, O, Y):
                    for s in r.free:
                        pool.sem_inc(s, 1)
                for m, val in ((lc[:, :, :, NB:NB + 4], LOWEST), (strike[:, :, :, 4:8], LOWEST), (bmax[:, :, :, :], 0.0),
                               (shift_l[:, :, :, 2:NB], 0.0), (pto[:, :, :, :], 0.0), (pad[:, 0:4], 0.0)):
                    g_.memset(m, val).then_inc(constants, 1)
                pool.sem_inc(armed, 1)
                pool.wait_ge(constants, 6)

                pool.wait_ge(units_in, 16 * 5)

                def pad_wait():
                    g_.tensor_tensor(pad[:, 2:3], pad[:, 3:4], pad[:, 3:4], ALU.add)

                def compressed(t):
                    Q.wait_read(pool, t, "lc")
                    done("lc_done", g_.tensor_tensor(lc[:, :, :, 0:NB], lc[:, :, :, 0:NB],
                                                     block_no[:, :, None, :].broadcast_to([P, TT, HG, NB]), ALU.add))

                def shifts(t):
                    need(pool, "top_done", t)
                    pad_wait()
                    done("strike_done", g_.tensor_copy(strike[:, :, :, 0:4], top[:, :, :, 0:4]))
                    done("pc_in", g_.tensor_tensor(pc[:, :, :, :], lc[:, :, :, 0:NB],
                                                   top[:, :, :, 0:1].broadcast_to([P, TT, HG, NB]), ALU.subtract))
                    need(pool, "smax_done", t)
                    done("shift_lo", g_.tensor_tensor(
                        shift_s[:, :, :, 0:NB - 1], unsel[:, :, :, 0:NB - 1],
                        smax_hi[:, :].rearrange("p (i h) -> p i h", i=TT)[:, :, :, None].broadcast_to([P, TT, HG, NB - 1]),
                        ALU.add))
                    need(pool, "cfac_done", t)
                    done("pc_done", g_.tensor_tensor(pc[:, :, :, :], pc[:, :, :, :],
                                                     cfac[:, :, :, None].broadcast_to([P, TT, HG, NB]), ALU.mult))

                def candidates(t, behind=None):
                    need(pool, "xy_in", t)
                    done("xy_done", g_.tensor_tensor(xy[:, :, :, :], xy[:, :, :, :], sim[:, :, :, :], ALU.add))
                    done("cand_done", g_.tensor_tensor(cand[:, :, :, :], t8[:, 0, :, :, None].broadcast_to([P, PH, 8, 8]),
                                                       t8[:, 1, :, None, :].broadcast_to([P, PH, 8, 8]), ALU.add))
                    need(pool, "xy_done", t)
                    for h in range(PH):
                        done("sum_done", g_.tensor_tensor(sumxy[:, h, :, :], xy[:, 0, h, 0:XK, None].broadcast_to([P, XK, KEYS]),
                                                          xy[:, 1, h, None, :].broadcast_to([P, XK, KEYS]), ALU.add))
                        if h == 0:
                            need(pool, "c8_done", t)
                            done("e8_in", g_.tensor_tensor(e8[:, :, :], c8[:, :, :], c8[:, :, 0:1].broadcast_to([P, PH, 8]),
                                                           ALU.subtract))
                            if behind:
                                silu_weights(behind)

                def weights(t):
                    for h in range(1, PH):
                        need(pool, "mw_done", t, h + 1)
                        if h > 1:
                            need(pool, "cw_sum", t, h - 1)
                        done("cw_sum", g_.tensor_tensor(cw[:, :], cw[:, :], mw[:, h % 2, :], ALU.add))

                def silu_weights(t):
                    need(pool, "clast_done", t)
                    F.wait_read(pool, t, "w0")
                    F.wait_read(pool, t, "w1")
                    done("cw_done", g_.tensor_tensor(cw[:, :], cw[:, :], sw[:, :], ALU.mult))

                def result_in(t):
                    loaded_by(pool, late_in, N_LATE, t)
                    done("xb_done", g_.tensor_tensor(xb[:, t.half, :], xb[:, t.half, :], bdb[:, :], ALU.add))

                def branches(t, hp):
                    if hp == 0:
                        need_before(pool, "st_at", t)
                    O.wait_read(pool, t, f"o{hp}")
                    k0, k1 = (on[:, hp, 2 * TT * k:2 * TT * (k + 1), :].rearrange("p (h i) d -> p i h d", h=2)
                              for k in range(2))
                    done("at_sum", g_.tensor_tensor(at[:, :, 2 * hp:2 * hp + 2, :], k0, k1, ALU.add))
                    if hp == 0:
                        return
                    need(pool, "at_sum", t)
                    K.wait_read(pool, t, "co")
                    done("at_done", g_.tensor_tensor(at[:, :, :, :].rearrange("p i h d -> p i (h d)"),
                                                     at[:, :, :, :].rearrange("p i h d -> p i (h d)"), co[:, :, :], ALU.add))

                def lead(n):
                    compressed(n)
                    candidates(n)
                    need(pool, "sum_done", n)
                    g_.tensor_copy(ko[SP3:P, :, :, :].rearrange("p a h t -> p (a h) t"),
                                   onehot[SP3:P, None, :].broadcast_to([P - SP3, 2 * HG, T])).then_inc(key_blocks, 1)
                    pool.wait_ge(key_blocks, 1)
                    shifts(n)

                def step(t):
                    n = None if t.tail else t.next()
                    weights(t)
                    if n:
                        compressed(n)
                    if n:
                        candidates(n, behind=t)
                    else:
                        silu_weights(t)
                    result_in(t)
                    branches(t, 0)
                    if n:
                        shifts(n)
                    branches(t, 1)
                steps(pool, step, lead)

            @block.scalar
            def _(act):
                s = nc.scalar
                act.wait_ge(armed, 1)
                act.wait_ge(constants, 6)

                def head(t, h):
                    slot = h % 2
                    if h < 2:
                        need_before(act, "pv", t, h + 3)
                    else:
                        need(act, "pv", t, h - 1)
                    for j in range(3):
                        K.wait_full(act, t, f"s{h}{j}")
                        bank = K.bank(f"s{h}{j}")
                        n = T - j * P
                        last = s.activation(pts[:, slot, OFFS[j]:OFFS[j] + n], bank[:, 0:n], ACT.Exp)
                        if j == 1:
                            last = s.activation(pts[0:112, slot, OFFS[3]:OFFS[3] + P], bank[0:112, n:n + P], ACT.Exp)
                        K.released(f"s{h}{j}", last)
                    if h < HG - 1:
                        head_shifts(t, h + 1)
                    K.wait_full(act, t, f"d{h}")
                    K.released(f"d{h}", s.activation(ptl[:, slot, :], K.bank(f"d{h}")[:, :], ACT.Exp))

                def expert(t, h):
                    need(act, "nmax_done", t)
                    need(act, "sum_done", t, h + 1)
                    if h >= 2:
                        need(act, "mw_done", t, h - 1)
                    done("ex_done", s.activation(ex[:, h % 2, :], sumxy[:, h, :, :].rearrange("p a b -> p (a b)"),
                                                 ACT.Exp, bias=nmax[:, h:h + 1]))

                def tanh(t, job, dst, name):
                    F.wait_full(act, t, job)
                    done(name, s.activation(dst, F.bank(job)[:, :], ACT.Tanh, scale=0.5))

                def key_scores(n):
                    F.wait_full(act, n, "sim")
                    F.released("sim", s.activation(sim[:, :, :, :].rearrange("p a h k -> p (a h k)"),
                                                   F.bank("sim")[:, :], ACT.Copy))

                def e8_exp(n):
                    need(act, "e8_in", n)
                    done("e8_exp", s.activation(e8[:, :, :], e8[:, :, :], ACT.Exp))

                def pc_exp(n):
                    need(act, "pc_in", n)
                    done("pc_exp", s.activation(pc[:, :, :, :], pc[:, :, :, :], ACT.Exp))

                def shifts(t):
                    K.wait_full(act, t, "aug")
                    K.released("aug", s.activation(shiftT[:, :], K.bank("aug")[:, :].bitcast(BF16)[:, 0:T], ACT.Copy))

                def head_shifts(t, h):
                    K.wait_full(act, t, f"a{h}")
                    K.released(f"a{h}", s.activation(qo[SP3:P, t.half, h, :], K.bank(f"a{h}")[SP3:P, :], ACT.Copy))

                def openings(t):
                    K.wait_full(act, t, "pcT")
                    K.released("pcT", s.activation(pcT[:, :], K.bank("pcT")[:, :], ACT.Copy))
                    expert(t, 2)
                    need_before(act, "pv", t)
                    K.wait_full(act, t, "off")
                    K.released("off", s.activation(pto[96:128, :, :, :].rearrange("p h i c -> p (h i c)"),
                                                   K.bank("off")[96:128, 0:384], ACT.Exp))
                    head_shifts(t, 0)
                    tanh(t, "g0", th[:, 0, :], "th_done")
                    need_before(act, "at_done", t)
                    K.wait_full(act, t, "co")
                    K.released("co", s.activation(co[:, :, :].rearrange("p i n -> p (i n)"),
                                                  K.bank("co")[:, 0:TT * HG * D], ACT.Copy))
                    expert(t, 3)

                def lead(n):
                    key_scores(n)
                    e8_exp(n)
                    pc_exp(n)

                def step(t):
                    n = None if t.tail else t.next()
                    tanh(t, "w0", tw[:, 0, :], "tw_done")
                    expert(t, 0)
                    tanh(t, "w1", tw[:, 1, :], "tw_done")
                    expert(t, 1)
                    shifts(t)
                    if n:
                        key_scores(n)
                    openings(t)
                    head(t, 0)
                    head(t, 1)
                    tanh(t, "g1", th[:, 1, :], "th_done")
                    head(t, 2)
                    if n:
                        e8_exp(n)
                    head(t, 3)
                    for j in range(2):
                        F.wait_full(act, t, f"t{j}")
                        F.released(f"t{j}", s.activation(cwT[:, 4 * j:4 * j + 4, :].rearrange("p e t -> p (e t)"),
                                                         F.bank(f"t{j}")[:, :], ACT.Copy))
                    if n:
                        pc_exp(n)
                steps(act, step, lead)

            @block.vector
            def _(dve):
                v = nc.vector
                dve.wait_ge(armed, 1)
                dve.wait_ge(constants, 6)
                cn = Chain(dve, near_chain, 10)
                cf = Chain(dve, far_chain, 10)

                def pad_wait():
                    v.memset(pad[:, 0:1], 0.0)

                def gate(t, j):
                    need(dve, "th_done", t, j + 1)
                    F.released(f"g{j}", v.scalar_tensor_tensor(gs[:, j, :], th[:, j, :], 1.0, F.bank(f"g{j}")[:, :],
                                                               ALU.add, ALU.mult))

                def up(t, j):
                    F.wait_read(dve, t, f"g{j}")
                    F.wait_full(dve, t, f"u{j}")
                    F.released(f"u{j}", v.tensor_tensor(hT[:, 4 * j:4 * j + 4, :].rearrange("p f t -> p (f t)"), gs[:, j, :],
                                                        F.bank(f"u{j}")[:, :], ALU.mult))

                def block_max(t, h, part):
                    job, tiles = ((f"p{h}3", ((3, 0),)), (f"p{h}0", ((0, 0), (2, P))), (f"p{h}1", ((1, 0),)))[part]
                    Q.wait_full(dve, t, job)
                    for i, o in tiles:
                        n = 8 * (i + 1)
                        last = v.tensor_reduce(bmax[:, i, h, 0:n],
                                               Q.bank(job)[:, o:o + n * BLK].rearrange("p (n j) -> p n j", j=BLK),
                                               AX.X, ALU.max)
                    Q.released(job, last)

                def compressed(t):
                    Q.wait_full(dve, t, "lc")
                    Q.released("lc", v.tensor_tensor(
                        lc[:, :, :, 0:NB], Q.bank("lc")[:, :].rearrange("p (i h n) -> p i h n", i=TT, h=HG),
                        block_ok[:, :, None, :].broadcast_to([P, TT, HG, NB]), ALU.mult))

                def best_blocks(t):
                    need(dve, "lc_done", t)
                    pad_wait()
                    for i in range(TT):
                        for h in range(HG):
                            last = v.max(top[:, i, h, :], lc[:, i, h, 0:NB])
                    done("top_done", last)

                def local_max(t):
                    for j in range(2):
                        Q.wait_full(dve, t, f"m{j}")
                        last = v.tensor_reduce(lmax[:, 8 * j:8 * j + 8], Q.bank(f"m{j}")[:, :].rearrange(
                            "p (n k) -> p n k", k=64), AX.X, ALU.max, negate=True)
                        Q.released(f"m{j}", last)

                def shifts(t):
                    need(dve, "strike_done", t)
                    pad_wait()
                    for i in range(TT):
                        for h in range(HG):
                            last = v.match_replace(struck[:, i, h, :], strike[:, i, h, :], lc[:, i, h, :], TAKEN)
                    cn.link(last)
                    cn.link(v.tensor_scalar(unsel[:, :, :, :], struck[:, :, :, 0:NB], TAKEN / 10, NEG, ALU.is_lt, ALU.mult))
                    cn.link(v.tensor_tensor(bsel[:, :, :, :], bmax[:, :, :, :], unsel[:, :, :, :], ALU.add))
                    cn.link(v.tensor_reduce(smax[:, :], bsel[:, :, :, :].rearrange("p i h n -> p (i h) n"), AX.X,
                                            ALU.max, negate=True))
                    done("smax_done", v.tensor_copy(smax_hi[:, :], smax[:, :]))
                    need(dve, "smax_done", t)
                    v.tensor_tensor(shift_s[:, :, :, NB - 1], smax[:, :].rearrange("p (i h) -> p i h", i=TT),
                                    smax_hi[:, :].rearrange("p (i h) -> p i h", i=TT), ALU.subtract)
                    lm = lmax[:, :].rearrange("p (h i) -> p i h", h=HG)
                    cn.link(v.tensor_copy(shift_l[:, :, :, 0], lm))
                    done("shift_done", v.tensor_tensor(shift_l[:, :, :, 1], lm, shift_l[:, :, :, 0], ALU.subtract))
                    need(dve, "pc_exp", t)
                    loaded_by(dve, late_in, N_LATE, t)
                    cn.link(v.tensor_reduce(csum[:, :], pc[:, :, :, :].rearrange("p i h n -> p (i h) n"), AX.X, ALU.add))
                    cn.link(v.reciprocal(csum[:, :], csum[:, :]))
                    done("cfac_done", v.tensor_tensor(cfac[:, :, :], csum[:, :].rearrange("p (i h) -> p i h", i=TT),
                                                      gt[:, t.half, :, 0:1].broadcast_to([P, TT, HG]), ALU.mult))

                def best_keys(t):
                    F.wait_read(dve, t, "sim")
                    pad_wait()
                    for a in range(2):
                        for h in range(PH):
                            last = v.max(t8[:, a, h, :], sim[:, a, h, :])
                    done("t8_done", last)
                    need(dve, "t8_done", t)
                    pad_wait()
                    for a in range(2):
                        for h in range(PH):
                            last = v.match_replace(marks[:, a, h, :], t8[:, a, h, :], sim[:, a, h, :], TAKEN)
                    cn.link(last)
                    done("xy_in", v.tensor_scalar(xy[:, :, :, :], marks[:, :, :, :], TAKEN / 10, NEG, ALU.is_lt, ALU.mult))

                def best_pairs(t):
                    need(dve, "cand_done", t)
                    pad_wait()
                    for h in range(PH):
                        last = v.max(c8[:, h, :], cand[:, h, :, :].rearrange("p a b -> p (a b)"))
                    done("c8_done", last)
                    need(dve, "c8_done", t)
                    done("nmax_done", v.tensor_scalar(nmax[:, :], c8[:, :, 0], -1.0, None, ALU.mult))

                def pair_sums(t):
                    need(dve, "e8_exp", t)
                    cn.link(v.tensor_reduce(esum[:, :], e8[:, :, :], AX.X, ALU.add))
                    cn.link(v.reciprocal(erec[:, :], esum[:, :]))

                def expert(t, h):
                    dst = cw[:, :] if h == 0 else mw[:, h % 2, :]
                    need(dve, "sum_done", t, h + 1)
                    if h == 3:
                        need(dve, "cw_sum", t, 1)
                    cf.link(v.tensor_scalar(dst, sumxy[:, h, :, :].rearrange("p a b -> p (a b)"), c8[:, h, 7:8],
                                            erec[:, h:h + 1], ALU.is_ge, ALU.mult))
                    need(dve, "ex_done", t, h + 1)
                    done("mw_done", v.tensor_tensor(dst, dst, ex[:, h % 2, :], ALU.mult))

                def last_expert(t):
                    need(dve, "cw_sum", t)
                    cf.link(v.tensor_reduce(csm[:, :], cw[:, :], AX.X, ALU.add))
                    cf.link(v.tensor_tensor(clast[:, :], cw[:, EX - 1:EX], csm[:, :], ALU.subtract))
                    done("clast_done", v.tensor_scalar(cw[:, EX - 1:EX], clast[:, :], float(PH), None, ALU.add))

                def expert_silu(t, j):
                    need(dve, "tw_done", t, j + 1)
                    F.released(f"w{j}", v.scalar_tensor_tensor(sw[:, 512 * j:512 * j + 512], tw[:, j, :], 1.0,
                                                               F.bank(f"w{j}")[:, :], ALU.add, ALU.mult))

                def normalize(t, hp):
                    need(dve, "pv", t, 2 * hp + 2)
                    bank = O.bank(f"o{hp}")[:, 0:4 * TT * VW].rearrange("p (n d) -> p n d", d=VW)
                    cf.link(v.reciprocal(rs[:, :], bank[:, :, D]))
                    cf.link(v.tensor_tensor(fs[:, :].rearrange("p (k h i) -> p k h i", k=2, h=2),
                                            rs[:, :].rearrange("p (k h i) -> p k h i", k=2, h=2),
                                            gt[:, t.half, :, 1:3].rearrange("p i k -> p k i")[:, :, None, :]
                                            .broadcast_to([P, 2, 2, TT]), ALU.mult))
                    if hp == 0:
                        need_before(dve, "at_done", t)
                    O.released(f"o{hp}", v.tensor_tensor(on[:, hp, :, :], bank[:, :, 0:D],
                                                         fs[:, :, None].broadcast_to([P, 4 * TT, D]), ALU.mult))

                def result(t):
                    Y.wait_full(dve, t, "y")
                    need_before(dve, "st_y", t)
                    need(dve, "xb_done", t)
                    Y.released("y", v.scalar_tensor_tensor(yo[:, :], Y.bank("y")[:, 0:C], 0.5, xb[:, t.half, :],
                                                           ALU.mult, ALU.add))

                def lead(n):
                    cn.start(n)
                    compressed(n)
                    for h in range(HG):
                        for part in range(3):
                            block_max(n, h, part)
                    best_keys(n)
                    best_pairs(n)
                    pair_sums(n)
                    best_blocks(n)
                    local_max(n)
                    shifts(n)
                    cn.end()

                def step(t):
                    n = None if t.tail else t.next()
                    cf.start(t)
                    expert_silu(t, 0)
                    expert(t, 0)
                    expert_silu(t, 1)
                    expert(t, 1)
                    if n:
                        cn.start(n)
                        compressed(n)
                    expert(t, 2)
                    gate(t, 0)
                    if n:
                        for part in range(3):
                            block_max(n, 0, part)
                    up(t, 0)
                    expert(t, 3)
                    if n:
                        for part in range(3):
                            block_max(n, 1, part)
                        best_keys(n)
                    gate(t, 1)
                    if n:
                        block_max(n, 2, 0)
                        block_max(n, 2, 1)
                    last_expert(t)
                    if n:
                        block_max(n, 2, 2)
                        best_pairs(n)
                    up(t, 1)
                    normalize(t, 0)
                    if n:
                        for part in range(3):
                            block_max(n, 3, part)
                        pair_sums(n)
                        best_blocks(n)
                        local_max(n)
                        shifts(n)
                        cn.end()
                    result(t)
                    normalize(t, 1)
                    cf.end()
                steps(dve, step, lead)

            @block.tensor
            def _(pe):
                mm, tr = nc.tensor.matmul, nc.tensor.transpose
                pe.wait_ge(armed, 1)
                pe.wait_ge(units_in, 16 * 5)
                pe.wait_ge(constants, 6)

                def up_rows(t, name, j, k):
                    w_, kind = (wfg, 0) if name == "g" else (wfu, 1)
                    if k == 0:
                        F.wait_free(pe, t, f"{name}{j}")
                        mm(F.bank(f"{name}{j}")[:, :], bias3[:, kind, j, :], tile_of[:, :, :].rearrange("r k t -> r (k t)"),
                           start=True, stop=True)
                    o = P * (4 * j + k)
                    dst = F.bank(f"{name}{j}")[:, k * P:k * P + P]
                    for c in range(2):
                        last = mm(dst, w_[:, c, o:o + P], xt[:, t.half, c, :], start=False, stop=(c == 1),
                                  skip_group_check=True)
                    if k == 3:
                        F.filled(f"{name}{j}", last)

                def token_rows(t, job, w_, o):
                    F.wait_free(pe, t, job)
                    for c in range(2):
                        last = mm(F.bank(job)[:, :], xt[:, t.half, c, :], w_[:, c, o:o + 512], start=(c == 0), stop=(c == 1))
                    F.filled(job, last)

                def queries(t, h, part):
                    job, tiles = ((f"p{h}3", ((3, 0),)), (f"p{h}0", ((0, 0), (2, P))), (f"p{h}1", ((1, 0),)))[part]
                    Q.wait_free(pe, t, job)
                    bank = Q.bank(job)
                    for i, o in tiles:
                        n = P * (i + 1)
                        last = mm(bank[:, o:o + n], qo[0:SP3, t.half, h, P * i:P * i + P], ko[0:SP3, t.half, h, 0:n],
                                  start=True, stop=(i > 0))
                        if i == 0:
                            last = mm(bank[:, 0:P], identb[:, :], causal_ts[:, :], start=False, stop=True)
                    Q.filled(job, last)

                def window(t, j):
                    job = f"m{j}"
                    Q.wait_free(pe, t, job)
                    bank = Q.bank(job)
                    mm(bank[:, :], identb[:, :], window_ts[:, None, :, :].broadcast_to([P, 2, TT, 64]),
                       start=True, stop=True)
                    for h2 in range(2):
                        h = 2 * j + h2
                        for i in range(TT):
                            for q in range(4):
                                s0 = P * i + 32 * q
                                o = 64 * (TT * h2 + i)
                                k_ = (ko[0:SP3, t.half, h, s0 - 32:s0 + 32] if s0 else
                                      ko[0:SP3, t.half, h, 0:32][:, None, :].broadcast_to([SP3, 2, 32]))
                                last = mm(bank[32 * q:32 * q + 32, o:o + 64], qo[0:SP3, t.half, h, s0:s0 + 32], k_,
                                          start=False, stop=True, skip_group_check=True)
                    Q.filled(job, last)

                def keys_rows(t, h, part):
                    if part == 0:
                        K.wait_read(pe, t, f"a{h}")
                    if part < 3:
                        job = f"s{h}{part}"
                        K.wait_free(pe, t, job)
                        bank = K.bank(job)
                        for i, o in (((0, 0),), ((1, 0), (3, 384)), ((2, 0),))[part]:
                            n, m = T - P * i, (P if i < 3 else 112)
                            last = mm(bank[0:m, o:o + n], ko[:, t.half, h, P * i:P * i + m], qo[:, t.half, h, P * i:T],
                                      start=True, stop=True)
                            if i == 0:
                                last = mm(bank[:, 0:64], identb[:, :], causal_st[:, :], start=False, stop=True,
                                          skip_group_check=True)
                    else:
                        job = f"d{h}"
                        K.wait_free(pe, t, job)
                        bank = K.bank(job)
                        mm(bank[:, :], identb[:, :], window_st[:, None, :].broadcast_to([P, TT, P]), start=True, stop=False)
                        for i in range(TT):
                            mm(bank[:, P * i:P * i + P], ko[0:SP3, t.half, h, P * i:P * i + P],
                               qo[0:SP3, t.half, h, P * i:P * i + P], start=False, stop=False)
                        last = mm(bank[:, :], headones[:, h, :], shiftT[:, :], start=False, stop=True)
                    K.filled(job, last)

                def values(t, h, part):
                    hp, h2 = divmod(h, 2)
                    slot = h % 2
                    bank = O.bank(f"o{hp}")
                    if part == 0:
                        if h2 == 0:
                            O.wait_free(pe, t, f"o{hp}")
                        for j in (1, 2):
                            K.wait_read(pe, t, f"s{h}{j}")
                    if part < 3:
                        for i in ((0, 1), (2,), (3,))[part]:
                            o = VW * (TT * h2 + i)
                            for j in range(i + 1):
                                m = P if j < 3 else 112
                                c = OFFS[j] + P * (i - j)
                                mm(bank[:, o:o + VW], pts[0:m, slot, c:c + P], vv[0:m, t.half, j, h, :],
                                   start=(j == 0), stop=(j == i))
                        return
                    K.wait_read(pe, t, f"d{h}")
                    if h == 0:
                        K.wait_read(pe, t, "off")
                    for i in range(TT):
                        o = VW * (2 * TT + TT * h2 + i)
                        last = mm(bank[:, o:o + VW], ptl[:, slot, P * i:P * i + P], vv[:, t.half, i, h, :],
                                  start=True, stop=True)
                        if i:
                            last = mm(bank[0:32, o:o + VW], pto[:, h, i - 1, :], vv[:, t.half, i - 1, h, :],
                                      start=False, stop=True, skip_group_check=True)
                    done("pv", last)

                def compressed(t):
                    Q.wait_free(pe, t, "lc")
                    loaded_by(pe, near_in, N_NEAR, t)
                    for i in range(TT):
                        last = mm(Q.bank("lc")[:, P * i:P * i + P], qf[:, t.half, P * i:P * i + P], kc[:, t.half, :],
                                  start=True, stop=True)
                    Q.filled("lc", last)

                def openings(t, part):
                    job = ("aug", "pcT", "off", "co")[part]
                    bank = K.bank(job)
                    if job == "aug":
                        need(pe, "shift_lo", t)
                        need(pe, "shift_done", t)
                        K.wait_free(pe, t, job)
                        for i in range(TT):
                            last = tr(bank[:, :].bitcast(BF16)[:, P * i:P * i + P],
                                      shift_l[:, i, :, :].rearrange("p h n -> p (h n)"), identb[:, :])
                    elif job == "pcT":
                        need(pe, "pc_done", t)
                        K.wait_free(pe, t, job)
                        for i in range(TT):
                            last = tr(bank[:, P * i:P * i + P], pc[:, i, :, :].rearrange("p h n -> p (h n)"), ident[:, :])
                    elif job == "off":
                        K.wait_free(pe, t, job)
                        mm(bank[96:128, 0:384], identb[:, 96:128], window_off[:, None, :].broadcast_to([P, 12, 32]),
                           start=True, stop=True)
                        for h in range(HG):
                            for i in range(TT - 1):
                                o = 32 * ((TT - 1) * h + i)
                                tq = slice(P * (i + 1), P * (i + 1) + 32)
                                mm(bank[96:128, o:o + 32], ko[0:SP3, t.half, h, P * i + 96:P * i + P], qo[0:SP3, t.half, h, tq],
                                   start=False, stop=False, skip_group_check=True)
                                last = mm(bank[96:128, o:o + 32], headones[:, h, 0:32], shiftT[:, tq], start=False,
                                          stop=True, skip_group_check=True)
                    else:
                        K.wait_free(pe, t, job)
                        loaded_by(pe, late_in, N_LATE, t)
                        for i in range(TT):
                            last = mm(bank[:, 64 * i:64 * i + 64], pcT[:, P * i:P * i + P], vc[:, t.half, :],
                                      start=True, stop=True)
                    K.filled(job, last)

                def head_shifts(t, h):
                    K.wait_free(pe, t, f"a{h}")
                    for i in range(TT):
                        last = mm(K.bank(f"a{h}")[SP3:P, P * i:P * i + P], shift_s[:, i, h, :], identb[:, :],
                                  start=True, stop=True)
                    K.filled(f"a{h}", last)

                def mlp_down(t, part):
                    if part == 0:
                        Y.wait_free(pe, t, "y")
                        F.wait_read(pe, t, "u1")
                    for f in (2 * part, 2 * part + 1):
                        mm(Y.bank("y")[:, 0:C], hT[:, f, :], wfd[:, f, :], start=(f == 0), stop=False)

                def transposed_weights(t):
                    need(pe, "cw_done", t)
                    for j in range(2):
                        F.wait_free(pe, t, f"t{j}")
                        for e in range(4):
                            o = P * (4 * j + e)
                            last = tr(F.bank(f"t{j}")[:, P * e:P * e + P], cw[:, o:o + P], ident[:, :])
                        F.filled(f"t{j}", last)

                def experts_down(t, j):
                    F.wait_read(pe, t, f"t{j}")
                    for e in range(4 * j, 4 * j + 4):
                        last = mm(Y.bank("y")[:, 0:C], cwT[:, e, :], wup[:, e, :], start=False, stop=(e == 7))
                    if j == 1:
                        Y.filled("y", last)

                def lead(n):
                    compressed(n)
                    token_rows(n, "sim", wsim, 0)
                    loaded_by(pe, parts_in, N_PARTS, n)
                    for h in range(HG):
                        for part in range(3):
                            queries(n, h, part)
                    window(n, 0)
                    window(n, 1)
                    pe.wait_ge(key_blocks, 1)

                def step(t):
                    n = None if t.tail else t.next()
                    token_rows(t, "w0", wdn, 0)
                    token_rows(t, "w1", wdn, 512)
                    if n:
                        compressed(n)
                    openings(t, 0)
                    if n:
                        token_rows(n, "sim", wsim, 0)
                        loaded_by(pe, parts_in, N_PARTS, n)
                    openings(t, 1)
                    up_rows(t, "g", 0, 0)
                    up_rows(t, "g", 0, 1)
                    openings(t, 2)
                    up_rows(t, "g", 0, 2)
                    head_shifts(t, 0)
                    up_rows(t, "g", 0, 3)
                    openings(t, 3)
                    for h in range(HG):
                        for part in range(4):
                            keys_rows(t, h, part)
                            if h < 3:
                                up_rows(t, "ugu"[h], (0, 1, 1)[h], part)
                            else:
                                mlp_down(t, part)
                            if n and part < 3:
                                queries(n, h, part)
                            if part == 2 and h < HG - 1:
                                head_shifts(t, h + 1)
                            if h > 0:
                                values(t, h - 1, part)
                    transposed_weights(t)
                    if n:
                        window(n, 0)
                    values(t, 3, 0)
                    experts_down(t, 0)
                    values(t, 3, 1)
                    if n:
                        window(n, 1)
                    values(t, 3, 2)
                    experts_down(t, 1)
                    values(t, 3, 3)
                steps(pe, step, lead)

        inner = ExitStack()
        with inner:
            sb, ps, sem = make(inner)
            wo = sb("wo", [P, 2, C])
            ar = sb("ar", [P, B, TT, C])
            yr = sb("yr", [P, B, TT, C])
            aT = sb("aT", [P, 2, 2, T])
            banks = [ps(f"fbank{i}", [P, 512]) for i in range(8)]
            R = Banks(banks, [sem(f"f_full{i}") for i in range(8)], [sem(f"f_free{i}") for i in range(8)],
                      ["a0", "a1", "o0", "o1"], front=["a0", "a1"])
            a_in = [sem(f"a_in{b}") for b in range(B)]
            y_in = [sem(f"y_in{b}") for b in range(B)]
            w_in = sem("wo_in")
            done = sem("res_stored")
            armed = sem("armed_f")

            def steps(step, lead):
                lead(Turn(0, 0, step=None))
                for b in range(B):
                    t = Turn(b // 2, b % 2, tail=(b == B - 1))
                    step(t, None if t.tail else t.next())

            block = inner.enter_context(nc.Block())

            @block.sync
            def _(sp):
                sp.dma_start(ar[:, 0, :, :], s_o[0].rearrange("i p c -> p i c")).then_inc(a_in[0], 16)
                sp.dma_start(wo[:, :, :], Wo.rearrange("(a p) n -> p a n", p=P)).then_inc(w_in, 16)
                for b in range(1, B):
                    sp.dma_start(ar[:, b, :, :], s_o[b].rearrange("i p c -> p i c")).then_inc(a_in[b], 16)

            @block.gpsimd
            def _(pool):
                for s in R.free[:4]:
                    pool.sem_inc(s, 1)
                pool.sem_inc(armed, 1)

            @block.tensor
            def _(pe):
                pe.wait_ge(armed, 1)

                def transposed(n):
                    pe.wait_ge(a_in[n.index], 16)
                    for c in range(2):
                        R.wait_free(pe, n, f"a{c}")
                        for i in range(TT):
                            last = nc.tensor.transpose(R.bank(f"a{c}")[:, i * P:i * P + P],
                                                       ar[:, n.index, i, c * P:c * P + P], ident[:, :])
                        R.filled(f"a{c}", last)

                def project(t):
                    for c in range(2):
                        R.wait_read(pe, t, f"a{c}")
                    for j in range(2):
                        R.wait_free(pe, t, f"o{j}")
                        for i in range(2):
                            for c in range(2):
                                last = nc.tensor.matmul(R.bank(f"o{j}")[:, i * C:i * C + C],
                                                        aT[:, t.half, c, (2 * j + i) * P:(2 * j + i + 1) * P], wo[:, c, :],
                                                        start=(c == 0), stop=(c == 1))
                        R.filled(f"o{j}", last)

                def step(t, n):
                    if n:
                        transposed(n)
                    project(t)
                pe.wait_ge(w_in, 16)
                steps(step, transposed)

            @block.scalar
            def _(act):
                ys = s_y.rearrange("(b i) p c -> b p i c", i=TT)
                for b in range(B):
                    act.dma_start(yr[:, b, :, :], ys[b]).then_inc(y_in[b], 16)
                act.wait_ge(armed, 1)
                ov = out.rearrange("b (i p) c -> b p i c", p=P)

                def transposed(n):
                    for c in range(2):
                        R.wait_full(act, n, f"a{c}")
                        R.released(f"a{c}", nc.scalar.activation(aT[:, n.half, c, :], R.bank(f"a{c}")[:, :], ACT.Copy))

                def step(t, n):
                    if n:
                        transposed(n)
                    R.wait_read(act, t, "o1")
                    act.dma_start(ov[t.index], yr[:, t.index, :, :]).then_inc(done, 16)
                steps(step, transposed)
                act.wait_ge(done, 16 * B)

            @block.vector
            def _(dve):
                dve.wait_ge(armed, 1)

                def step(t, n):
                    dve.wait_ge(y_in[t.index], 16)
                    for j in range(2):
                        R.wait_full(dve, t, f"o{j}")
                        part = yr[:, t.index, 2 * j:2 * j + 2, :]
                        R.released(f"o{j}", nc.vector.tensor_tensor(
                            part, R.bank(f"o{j}")[:, :].rearrange("p (i c) -> p i c", i=2), part, ALU.add))
                steps(step, lambda n: None)


_INS = ["L0_attn_x", "L0_attn_Wq", "L0_attn_Wk", "L0_attn_Wv", "L0_attn_Wo", "L0_attn_Wck", "L0_attn_Wcv",
        "L0_attn_Wg", "L0_attn_bg", "L0_ffn_Wg", "L0_ffn_bg", "L0_ffn_Wu", "L0_ffn_bu", "L0_ffn_Wd", "L0_ffn_bd",
        "L0_ffn_Wq", "L0_ffn_keys", "L0_ffn_down_embed", "L0_ffn_up_embed"]


def kernel(**inputs):
    import numpy as _np
    import concourse.bacc as _bacc
    from concourse import mybir as _mybir
    from concourse.bass_utils import run_bass_kernel_spmd as _run

    nc = _bacc.Bacc("TRN2", target_bir_lowering=False, num_devices=1)
    arrays, args = {}, []
    for name in _INS:
        a = _np.ascontiguousarray(inputs[name])
        arrays[f"in_{name}_dram"] = a
        args.append(nc.dram_tensor(f"in_{name}_dram", a.shape, _mybir.dt.from_np(a.dtype), kind="ExternalInput").ap())
    args.append(nc.dram_tensor("out_0_dram", (B, T, C), _mybir.dt.float32, kind="ExternalOutput").ap())
    build(nc, *args)
    r = _run(nc, [arrays], core_ids=[0])
    return r.results[0]["out_0_dram"]
```
